# Optimizing a Trainium2 kernel written in Bass

```python
import numpy as np
import jax
import jax.numpy as jnp

def _softmax(x, axis=-1):
    return jax.nn.softmax(x, axis=axis)

def _gelu(x):
    return jax.nn.gelu(x, approximate=True)

def _silu(x):
    return jax.nn.silu(x)

def _sigmoid(x):
    return jax.nn.sigmoid(x)

def _layernorm(x, axis=-1, eps=1e-05):
    m = jnp.mean(x, axis=axis, keepdims=True)
    v = jnp.var(x, axis=axis, keepdims=True)
    return (x - m) / jnp.sqrt(v + eps)

def _scatter_add(tgt, idx, src, axis=0):
    return tgt.at[idx].add(src)

def _segment_sum(src, seg, n):
    return jax.ops.segment_sum(src, seg, n)
kernel_name = 'mk_decoder_preln_d1_seqx_r8_c416c8'

def setup_inputs(seed: int=0):
    np.random.seed(seed)
    _w = jnp.asarray

    def _rec_inputs():
        import jax
        import jax.numpy as jnp
        _rk = jax.random.key(seed)
        x = -0.0002928 + 1 * jax.random.normal(jax.random.fold_in(_rk, 1), (64, 64, 128), jnp.float32)
        _lenS = 64 - jax.random.randint(jax.random.fold_in(_rk, 7), (64,), 0, max(1, 64 // 4) + 1, jnp.int32)
        _lenS2 = 64 - jax.random.randint(jax.random.fold_in(_rk, 8), (64,), 0, max(1, 64 // 4) + 1, jnp.int32)
        _ctx_1024P = jax.random.normal(jax.random.fold_in(_rk, 11), (64, 16, 128), jnp.float32)
        _ctx_1024c = jax.random.dirichlet(jax.random.fold_in(_rk, 511), 0.3 * jnp.ones((16,), jnp.float32), (64, 64))
        _ctx_1024t = jnp.einsum('bsk,bkd->bsd', _ctx_1024c, _ctx_1024P)
        _ctx_1024t = _ctx_1024t * jax.lax.rsqrt(jnp.mean(jnp.square(_ctx_1024t)) + 1e-12) * 0.953939
        ctx_1024 = -1.39393e-06 + 0.999914 * (_ctx_1024t + 0.3 * jax.random.normal(jax.random.fold_in(_rk, 611), (64, 64, 128), jnp.float32))
        _validS = jnp.arange(64)[None, :] < _lenS[:, None]
        _validS2 = jnp.arange(64)[None, :] < _lenS2[:, None]
        _causal = jnp.tril(jnp.ones((64, 64), dtype=bool))
        mask_BxSxS2_if1 = jnp.where(jnp.ones((64, 64, 64), dtype=bool), 1, 0).astype(jnp.int32)
        return (x, ctx_1024, mask_BxSxS2_if1)
    x, ctx_1024, mask_BxSxS2_if1 = _rec_inputs()

    def _L0_attn_setup():
        import jax, jax.numpy as jnp
        import numpy as np
        B, S, D, H = (2, 256, 128, 16)
        HD = D // H

        def _rope_tables(seq_len, dim):
            inv_freq = 1.0 / 10000.0 ** (jnp.arange(0, dim, 2, dtype=jnp.float32) / dim)
            t = jnp.arange(seq_len, dtype=jnp.float32)
            freqs = jnp.einsum('i,j->ij', t, inv_freq)
            emb = jnp.concatenate([freqs, freqs], axis=-1)
            return (jnp.cos(emb)[None, None], jnp.sin(emb)[None, None])

        def _rotate_half(x):
            x1, x2 = (x[..., :x.shape[-1] // 2], x[..., x.shape[-1] // 2:])
            return jnp.concatenate([-x2, x1], axis=-1)
        key = jax.random.key(seed)
        ks = jax.random.split(key, 5)
        sc = 1.0 / np.sqrt(D)
        return {'x': jax.random.normal(ks[0], (B, S, D), jnp.float32), 'wq': jax.random.normal(ks[1], (D, D), jnp.float32) * sc, 'bq': jnp.zeros((D,), jnp.float32), 'wk': jax.random.normal(ks[2], (D, D), jnp.float32) * sc, 'bk': jnp.zeros((D,), jnp.float32), 'wv': jax.random.normal(ks[3], (D, D), jnp.float32) * sc, 'bv': jnp.zeros((D,), jnp.float32), 'wo': jax.random.normal(ks[4], (D, D), jnp.float32) * sc, 'bo': jnp.zeros((D,), jnp.float32)}
    _L0_attn_all = _L0_attn_setup()
    _L0_attn_in = {k: v for k, v in _L0_attn_all.items() if k in ('wq', 'bq', 'wk', 'bk', 'wv', 'bv', 'wo', 'bo')}
    del _L0_attn_all

    def _L0_xattn_setup():
        import jax, jax.numpy as jnp
        import numpy as np
        B, S, D, H = (2, 256, 128, 16)
        DH = D // H
        key = jax.random.key(seed)
        ks = jax.random.split(key, 12)
        sc = 0.02
        return {'query': jax.random.normal(ks[0], (B, S, D), jnp.float32), 'key': jax.random.normal(ks[1], (B, S, D), jnp.float32), 'value': jax.random.normal(ks[2], (B, S, D), jnp.float32), 'mask': jnp.ones((B, S, S), jnp.int32), 'qw': jax.random.normal(ks[3], (D, D), jnp.float32) * sc, 'qb': jnp.zeros((D,), jnp.float32), 'kw': jax.random.normal(ks[4], (D, D), jnp.float32) * sc, 'kb': jnp.zeros((D,), jnp.float32), 'vw': jax.random.normal(ks[5], (D, D), jnp.float32) * sc, 'vb': jnp.zeros((D,), jnp.float32), 'ow': jax.random.normal(ks[6], (D, D), jnp.float32) * sc, 'ob': jnp.zeros((D,), jnp.float32)}
    _L0_xattn_all = _L0_xattn_setup()
    _L0_xattn_in = {k: v for k, v in _L0_xattn_all.items() if k in ('qw', 'qb', 'kw', 'kb', 'vw', 'vb', 'ow', 'ob')}
    del _L0_xattn_all

    def _L0_ffn_setup():
        import jax, jax.numpy as jnp
        import numpy as np
        E, D, F = (8, 128, 512)
        LN_EPS = 1e-05
        key = jax.random.key(seed)
        k = jax.random.split(key, 8)
        x = jax.random.normal(k[0], (4, 256, D), jnp.float32)
        centroids = jax.random.normal(k[1], (E, D), jnp.float32) * 0.1
        ln_g = jnp.ones((E, D), jnp.float32)
        ln_b = jnp.zeros((E, D), jnp.float32)
        w1 = jax.random.normal(k[2], (E, F, D), jnp.float32) * (1.0 / np.sqrt(D))
        b1 = jnp.zeros((E, F), jnp.float32)
        w2 = jax.random.normal(k[3], (E, D, F), jnp.float32) * (1.0 / np.sqrt(F))
        b2 = jnp.zeros((E, D), jnp.float32)
        return {'input_features': x, 'centroids': centroids, 'ln_g': ln_g, 'ln_b': ln_b, 'w1': w1, 'b1': b1, 'w2': w2, 'b2': b2}
    _L0_ffn_all = _L0_ffn_setup()
    _L0_ffn_in = {k: v for k, v in _L0_ffn_all.items() if k in ('centroids', 'ln_g', 'ln_b', 'w1', 'b1', 'w2', 'b2')}
    del _L0_ffn_all
    return {'x': x, 'ctx_1024': ctx_1024, 'mask_BxSxS2_if1': mask_BxSxS2_if1, 'L0_attn_wq': _L0_attn_in['wq'], 'L0_attn_bq': _L0_attn_in['bq'], 'L0_attn_wk': _L0_attn_in['wk'], 'L0_attn_bk': _L0_attn_in['bk'], 'L0_attn_wv': _L0_attn_in['wv'], 'L0_attn_bv': _L0_attn_in['bv'], 'L0_attn_wo': _L0_attn_in['wo'], 'L0_attn_bo': _L0_attn_in['bo'], 'L0_xattn_qw': _L0_xattn_in['qw'], 'L0_xattn_qb': _L0_xattn_in['qb'], 'L0_xattn_kw': _L0_xattn_in['kw'], 'L0_xattn_kb': _L0_xattn_in['kb'], 'L0_xattn_vw': _L0_xattn_in['vw'], 'L0_xattn_vb': _L0_xattn_in['vb'], 'L0_xattn_ow': _L0_xattn_in['ow'], 'L0_xattn_ob': _L0_xattn_in['ob'], 'L0_ffn_centroids': _L0_ffn_in['centroids'], 'L0_ffn_ln_g': _L0_ffn_in['ln_g'], 'L0_ffn_ln_b': _L0_ffn_in['ln_b'], 'L0_ffn_w1': _L0_ffn_in['w1'], 'L0_ffn_b1': _L0_ffn_in['b1'], 'L0_ffn_w2': _L0_ffn_in['w2'], 'L0_ffn_b2': _L0_ffn_in['b2']}

def reference(x, ctx_1024, mask_BxSxS2_if1, L0_attn_wq, L0_attn_bq, L0_attn_wk, L0_attn_bk, L0_attn_wv, L0_attn_bv, L0_attn_wo, L0_attn_bo, L0_xattn_qw, L0_xattn_qb, L0_xattn_kw, L0_xattn_kb, L0_xattn_vw, L0_xattn_vb, L0_xattn_ow, L0_xattn_ob, L0_ffn_centroids, L0_ffn_ln_g, L0_ffn_ln_b, L0_ffn_w1, L0_ffn_b1, L0_ffn_w2, L0_ffn_b2):
    import jax
    import jax.numpy as jnp

    def _L0_attn_ref(x, wq, bq, wk, bk, wv, bv, wo, bo):
        import jax, jax.numpy as jnp
        import numpy as np
        B, S, D, H = (2, 256, 128, 16)
        HD = D // H

        def _rope_tables(seq_len, dim):
            inv_freq = 1.0 / 10000.0 ** (jnp.arange(0, dim, 2, dtype=jnp.float32) / dim)
            t = jnp.arange(seq_len, dtype=jnp.float32)
            freqs = jnp.einsum('i,j->ij', t, inv_freq)
            emb = jnp.concatenate([freqs, freqs], axis=-1)
            return (jnp.cos(emb)[None, None], jnp.sin(emb)[None, None])

        def _rotate_half(x):
            x1, x2 = (x[..., :x.shape[-1] // 2], x[..., x.shape[-1] // 2:])
            return jnp.concatenate([-x2, x1], axis=-1)
        b, s, d = x.shape
        h, hd = (H, d // H)

        def proj(w, bias):
            return (x @ w.T + bias).reshape(b, s, h, hd).transpose(0, 2, 1, 3)
        q, k, v = (proj(wq, bq), proj(wk, bk), proj(wv, bv))
        cos, sin = _rope_tables(s, hd)
        q = q * cos + _rotate_half(q) * sin
        k = k * cos + _rotate_half(k) * sin
        scores = jnp.einsum('bhqd,bhkd->bhqk', q, k) / jnp.sqrt(jnp.float32(hd))
        attn = jax.nn.softmax(scores, axis=-1)
        out = jnp.einsum('bhqk,bhkd->bhqd', attn, v)
        out = out.transpose(0, 2, 1, 3).reshape(b, s, d)
        return out @ wo.T + bo

    def _L0_xattn_ref(query, key, value, mask, qw, qb, kw, kb, vw, vb, ow, ob):
        import jax, jax.numpy as jnp
        import numpy as np
        B, S, D, H = (2, 256, 128, 16)
        DH = D // H
        q = query @ qw.T + qb
        k = key @ kw.T + kb
        v = value @ vw.T + vb

        def split(x):
            b, s, _ = x.shape
            return x.reshape(b, s, H, DH).transpose(0, 2, 1, 3)
        qh, kh, vh = (split(q), split(k), split(v))
        scale = DH ** (-0.5)
        scores = jnp.einsum('bhqd,bhkd->bhqk', qh * scale, kh)
        scores = jnp.where(mask[:, None] == 0, jnp.float32(-1000000000.0), scores)
        probs = jax.nn.softmax(scores, axis=-1)
        out = jnp.einsum('bhqk,bhkd->bhqd', probs, vh)
        out = out.transpose(0, 2, 1, 3).reshape(out.shape[0], -1, H * DH)
        return out @ ow.T + ob

    def _L0_ffn_ref(input_features, centroids, ln_g, ln_b, w1, b1, w2, b2):
        import jax, jax.numpy as jnp
        import numpy as np
        E, D, F = (8, 128, 512)
        LN_EPS = 1e-05
        x = input_features.reshape(-1, D)
        aff = jax.lax.stop_gradient(x) @ centroids.T
        assign = jnp.argmax(aff, axis=1)
        onehot = jax.nn.one_hot(assign, E, dtype=x.dtype)
        mu = jnp.mean(x, axis=-1, keepdims=True)
        var = jnp.mean((x - mu) ** 2, axis=-1, keepdims=True)
        xhat = (x - mu) * jax.lax.rsqrt(var + LN_EPS)
        xn = xhat[None, :, :] * ln_g[:, None, :] + ln_b[:, None, :]
        h = jax.nn.relu(jnp.einsum('etd,efd->etf', xn, w1) + b1[:, None, :])
        y = x[None, :, :] + jnp.einsum('etf,edf->etd', h, w2) + b2[:, None, :]
        alpha = jax.nn.sigmoid(x @ centroids.T)
        a = alpha.T[:, :, None]
        gated = a * y + (1.0 - a) * x[None, :, :]
        out = jnp.einsum('te,etd->td', onehot, gated)
        return out.reshape(input_features.shape)
    x = x + _L0_attn_ref(_layernorm(x, axis=-1), L0_attn_wq, L0_attn_bq, L0_attn_wk, L0_attn_bk, L0_attn_wv, L0_attn_bv, L0_attn_wo, L0_attn_bo)
    x = x + _L0_xattn_ref(_layernorm(x, axis=-1), ctx_1024, ctx_1024, mask_BxSxS2_if1, L0_xattn_qw, L0_xattn_qb, L0_xattn_kw, L0_xattn_kb, L0_xattn_vw, L0_xattn_vb, L0_xattn_ow, L0_xattn_ob)
    x = x + _L0_ffn_ref(_layernorm(x, axis=-1), L0_ffn_centroids, L0_ffn_ln_g, L0_ffn_ln_b, L0_ffn_w1, L0_ffn_b1, L0_ffn_w2, L0_ffn_b2)
    return x

_drawn_inputs = setup_inputs


def setup_inputs(seed=0):
    import zlib

    import numpy as np

    out = dict(_drawn_inputs(seed))
    spreads = {'L0_attn_bq': (0.0, 0.1),
     'L0_attn_bk': (0.0, 0.1),
     'L0_attn_bv': (0.0, 0.1),
     'L0_attn_bo': (0.0, 0.1),
     'L0_xattn_qb': (0.0, 0.8),
     'L0_xattn_kb': (0.0, 0.8),
     'L0_xattn_vb': (0.0, 0.1),
     'L0_xattn_ob': (0.0, 0.1),
     'L0_ffn_ln_g': (1.0, 0.2),
     'L0_ffn_ln_b': (0.0, 0.283),
     'L0_ffn_b1': (0.0, 0.29),
     'L0_ffn_b2': (0.0, 0.1)}
    factors = {'L0_xattn_qw': 8.0, 'L0_xattn_kw': 6.745}
    for name, (base, spread) in spreads.items():
        noise = np.random.default_rng([zlib.crc32(name.encode()), seed]).standard_normal(out[name].shape)
        drawn = base * np.exp(spread * noise) if base else spread * noise
        out[name] = jnp.asarray(drawn.astype(out[name].dtype))
    for name, factor in factors.items():
        out[name] = (out[name] * factor).astype(out[name].dtype)
    return out
```

```python
import concourse.bass as bass
from concourse import mybir
from contextlib import ExitStack

B, S, D, H = 64, 64, 128, 16
HD = D // H
E, F = 8, 512
P = 128
T = B * S
NT = T // P
CHUNK = 512
UNITS = CHUNK // P
SEQS = CHUNK // S
NCH = T // CHUNK
GROUPS = 4
GH = H // GROUPS
PAIRS = H // 2
STK = 96
FC = F // P
FT = 40
EPS = 1e-5
MASKED = -2.0 ** 40
SCALE = HD ** -0.5
WCOLS = F + F + FC + D

PH = 4
ITERS = NCH // 2

C_ID, C_TRI, C_COS, C_SIN = 0, 128, 256, 320
C_MASK = 384
C_RANK = 388
C_SEG = 396
C_IOTA = C_SEG + E * NT
C_END = C_IOTA + FT

(WQ, WQR, WK, WKR, WV, WO, XQ, XK, XV, XO) = range(10)


def decoder_layer(nc, x, ctx_in, mask_q, mask_k, wts, bias_cols, bv_cols, bo_rows, consts, centro, ln_g, ln_b,
                  w1t, w2t, b1c, b2, out):
    f32, f16, bf16, i32 = mybir.dt.float32, mybir.dt.float16, mybir.dt.bfloat16, mybir.dt.int32
    ALU, ACT, AX = mybir.AluOpType, mybir.ActivationFunctionType, mybir.AxisListType

    es = ExitStack()
    with es:
        def sb(name, shape, dt=f32):
            return es.enter_context(nc.sbuf_tensor(name, shape, dt))

        def sem(name):
            return es.enter_context(nc.semaphore(name))

        xs_dram = nc.dram_tensor("sorted_in", (FT * P, D), f32, kind="Internal").ap()
        ys_dram = nc.dram_tensor("sorted_out", (FT * P, D), f32, kind="Internal").ap()

        cst = sb("cst", [P, C_END])
        ident = cst[:, C_ID:C_ID + P]
        tri = cst[:, C_TRI:C_TRI + P]
        negid = sb("negid", [P, P], bf16)
        idb = sb("idb", [P, P], bf16)
        dupid = [sb(f"dupid{b}", [P, 2, S], bf16) for b in range(2)]
        sel16 = sb("sel16", [P, 2, 2, GROUPS, STK], f16)
        ones = sb("ones", [P, P])
        minus_half = sb("minus_half", [P, NT])
        eps_col = sb("eps_col", [P, UNITS])
        w = sb("w", [P, 10, P])
        bcol = sb("bcol", [P, 6])
        bvc = sb("bvc", [P, 2])
        bor = sb("bor", [1, 2, D])
        bo_eff = sb("bo_eff", [P, 2, D])
        cT = sb("cT", [P, E])
        lng = sb("lng", [P, E])
        lnb = sb("lnb", [P, E])
        w1raw = sb("w1raw", [P, E, F])
        wpack = sb("wpack", [P, E, WCOLS])
        b1raw = sb("b1raw", [P, E, FC])

        xin = [sb(f"xin{i}", [P, UNITS, D]) for i in range(2)]
        cin = [sb(f"cin{i}", [P, UNITS, D]) for i in range(2)]
        x1 = [sb(f"x1_{i}", [P, UNITS, D]) for i in range(2)]
        xb = [sb(f"xb{i}", [P, UNITS, D]) for i in range(2)]
        stack_mem = sb("stack_mem", [P, 3 * GROUPS * CHUNK], f16)
        *qs, ks = [stack_mem[0:STK, i * GROUPS * CHUNK:(i + 1) * GROUPS * CHUNK].rearrange("p (g t) -> p g t", g=GROUPS)
                   for i in range(3)]
        kbd_mem = [sb(f"kbd{i}", [P, GROUPS * GH * CHUNK], f16) for i in range(2)]
        kbd = [m[0:STK, :].rearrange("p (g b s t) -> p g b s t", g=GROUPS, b=SEQS, s=GH) for m in kbd_mem]
        v9 = [sb(f"v9_{i}", [P, SEQS, PAIRS, 2, HD + 1]) for i in range(2)]
        mraw = [sb(f"mraw{i}", [P, 2, UNITS, S], i32) for i in range(2)]
        madd = [sb(f"madd{i}", [P, 2, UNITS, S], bf16) for i in range(2)]
        stats = sb("stats", [P, UNITS, 6])
        mv = sb("mv", [P, UNITS, 2])
        ve = sb("ve", [P, UNITS])
        scratch = sb("scratch", [P, 1])
        rstd = sb("rstd", [P, UNITS])
        xn = sb("xn", [P, UNITS, D])
        xnT = sb("xnT", [P, SEQS, 2, S])
        cxT = sb("cxT", [P, SEQS, 2, S])
        t_sin = [sb(f"t_sin{i}", [P, CHUNK]) for i in range(2)]
        p32 = [sb(f"p32_{i}", [P, CHUNK]) for i in range(2)]
        phi = [sb(f"phi{i}", [P, CHUNK], f16) for i in range(2)]
        plo = [sb(f"plo{i}", [P, CHUNK], f16) for i in range(2)]
        mx = [sb(f"mx{i}", [P, H], bf16) for i in range(2)]
        prob = [sb(f"prob{i}", [P, PAIRS * S]) for i in range(4)]
        rden = sb("rden", [P, H])
        on = sb("on", [P, H, HD])
        onT = sb("onT", [P, P])
        late = [stack_mem[:, :].bitcast(f32), kbd_mem[1][:, 2 * WCOLS:].bitcast(f32)]

        def late_sb(i, *dims):
            size = 1
            for d in dims:
                size *= d
            got, late[i] = late[i][:, 0:size], late[i][:, size:]
            return got if len(dims) == 1 else got.rearrange("p (a b) -> p a b", a=dims[0])

        x2 = sb("x2", [P, NT, D])
        base = w1raw[:, :, :].rearrange("p e f -> p (e f)").rearrange("p (t d) -> p t d", d=D)
        xhat = sb("xhat", [P, NT, D])
        stat3 = late_sb(0, NT, 6)
        mv3 = sb("mv3", [P, NT, 2])
        r1 = sb("r1", [P, NT])
        r2 = sb("r2", [P, NT])
        rtmp = sb("rtmp", [P, NT])
        xl = [late_sb(0, D) for i in range(4)]
        xlT = [late_sb(0, P) for i in range(4)]
        aff = late_sb(1, NT, E)
        amax = late_sb(0, NT)
        alpha = late_sb(0, NT)
        eq = late_sb(1, NT, E)
        sel = late_sb(0, NT)
        oh = late_sb(1, E, NT)
        pre = late_sb(1, E, NT)
        tot = late_sb(1, E, NT)
        inc = late_sb(1, E, NT)
        gt = late_sb(0, NT)
        gt2 = late_sb(1, E, NT)
        ntile = sb("ntile", [P, E])
        tinc = sb("tinc", [P, E])
        texc = sb("texc", [P, E])
        posf = late_sb(0, NT)
        pos = sb("pos", [P, NT], i32)
        geq = late_sb(1, FT, E)
        etf = late_sb(0, FT)
        et = sb("et", [P, FT], i32)
        wb = [kbd_mem[i // 3][:, (i % 3) * 2 * WCOLS:(i % 3 + 1) * 2 * WCOLS].bitcast(f32) for i in range(4)]
        xt = [late_sb(0, D) for i in range(4)]
        xtT = [late_sb(1, P) for i in range(2)]
        hT = [late_sb(i, FC, P) for i in range(2)]
        yt = [late_sb(0, D) for i in range(4)]

        bank = [es.enter_context(nc.psum_tensor(f"bank{i}", [P, 512], f32)) for i in range(8)]
        bankA, bankB, bankO, bankY, bankP = bank[0:2], bank[2:4], bank[4], bank[5], bank[6:8]

        w_in, x_in, c_in = sem("w_in"), [sem("x_in0"), sem("x_in1")], [sem("c_in0"), sem("c_in1")]
        m_in, madd_ok = [sem("m_in0"), sem("m_in1")], sem("madd_ok")
        ffw_in = sem("ffw_in")
        sel_zero = sem("sel_zero")
        setup_dve, setup_pool = sem("setup_dve"), sem("setup_pool")
        v9_zero, v9_ok = sem("v9_zero"), sem("v9_ok")
        bo_mm, bo_done = sem("bo_mm"), sem("bo_done")
        spare, ln_own, ln_stats, rstd_own, rstd_ok = sem("spare"), sem("ln_own"), sem("ln_stats"), sem("rstd_own"), sem("rstd_ok")
        xn_ok, xb_ok = sem("xn_ok"), sem("xb_ok")
        p_mm, p_read = sem("p_mm"), [sem("p_read0"), sem("p_read1")]
        rope_ok, hi_ok, lo_ok = sem("rope_ok"), sem("hi_ok"), sem("lo_ok")
        kbd_ok = sem("kbd_ok")
        a_mm, mx_ok, b_mm, exp_ok, pv_mm = sem("a_mm"), sem("mx_ok"), sem("b_mm"), sem("exp_ok"), sem("pv_mm")
        rden_ok, on_ok, ot_mm, ot_ok, wo_mm, res_ok = (sem("rden_ok"), sem("on_ok"), sem("ot_mm"), sem("ot_ok"),
                                                       sem("wo_mm"), sem("res_ok"))

        b1_mm, b1_ok = sem("b1_mm"), sem("b1_ok")
        mv3_own, mv3_ok, r_own, r_ok = sem("mv3_own"), sem("mv3_ok"), sem("r_own"), sem("r_ok")
        xl_ok, xlT_mm, xlT_ok, aff_mm, aff_ok = sem("xl_ok"), sem("xlT_mm"), sem("xlT_ok"), sem("aff_mm"), sem("aff_ok")
        xhat_ok, base_ok = sem("xhat_ok"), sem("base_ok")
        route, amax_ok, sig_ok, oh_ok, rank_mm, rank_ok, et_ok = (sem("route"), sem("amax_ok"), sem("sig_ok"), sem("oh_ok"),
                                                                  sem("rank_mm"), sem("rank_ok"), sem("et_ok"))
        zeroed, scattered, scaled = sem("zeroed"), sem("scattered"), sem("scaled")
        wb_in = [sem(f"wb_in{r}") for r in range(4)]
        xt_in = [sem(f"xt_in{r}") for r in range(4)]
        yt_out = [sem(f"yt_out{r}") for r in range(4)]
        xtT_mm, xtT_ok, h_mm, relu_act, relu_dve, y_mm, y_ok = (sem("xtT_mm"), sem("xtT_ok"), sem("h_mm"), sem("relu_act"),
                                                                sem("relu_dve"), sem("y_mm"), sem("y_ok"))
        yg_in = [sem(f"yg_in{c}") for c in range(NT // 4)]
        out_ok, out_done = sem("out_ok"), sem("out_done")
        FU = 8
        wflat = wpack[:, :, :].rearrange("p e c -> p (e c)")

        START = 1
        EXP0, PV0 = 2, 4
        XLT0, AFF0, AFM0, XT0, RELU0, Y0 = 2, 2, 4, 2, 2, 4

        STEPS_SELF = [[[], []], [["T"], ["K", "Kr"]], [["Q", "Qr"], ["SK0", "SK1", "SK2", "SK3"]],
                      [["SQ0", "SQ1", "SQ2", "SQ3"], ["V0", "V1"]]]
        STEPS_CROSS = [[[], []], [["T", "C"], ["K"]], [["Q"], ["SK0", "SK1", "SK2", "SK3"]],
                       [["SQ0", "SQ1", "SQ2", "SQ3"], ["V0", "V1"]]]
        SELF_ITEMS = [n for step in STEPS_SELF for part in step for n in part]
        CROSS_ITEMS = [n for step in STEPS_CROSS for part in step for n in part]

        def items(k):
            return SELF_ITEMS if k % PH < 2 else CROSS_ITEMS

        def step_items(k, u, after):
            return (STEPS_SELF if k % PH < 2 else STEPS_CROSS)[u][after]

        BODY_USES = 2 * len(SELF_ITEMS) + 2 * len(CROSS_ITEMS)

        def place(k, item):
            return sum(len(items(j)) for j in range(k)) + items(k).index(item)

        def pbank(k, item):
            return place(k, item) % 2

        def written(it, k, item):
            return it * BODY_USES + (place(k, item) + 1)

        def earlier_read(it, k, item):
            return it * (BODY_USES // 2) + place(k, item) // 2

        def read_out(it, k, item):
            return it * (BODY_USES // 2) + (place(k, item) // 2 + 1)

        block = es.enter_context(nc.Block())

        @block.sync
        def _(sp):
            def load_x(row, k):
                sp.dma_start(xin[k % 2][:, :, :],
                             x[bass.ds(row, CHUNK), :].rearrange("(u p) d -> p u d", p=P)).then_inc(x_in[k % 2], 16)

            def load_ctx(row, k):
                sp.dma_start(cin[k % 2][:, :, :],
                             ctx_in[bass.ds(row, CHUNK), :].rearrange("(u p) d -> p u d", p=P)).then_inc(c_in[k % 2], 16)

            def load_masks(row, k):
                for side, m in enumerate((mask_q, mask_k)):
                    sp.dma_start(mraw[k % 2][:, side, :, :],
                                 m[bass.ds(row, CHUNK), :].rearrange("(u p) s -> p u s", p=P)).then_inc(m_in[k % 2], 16)

            sp.dma_start(cst[:, :], consts).then_inc(w_in, 16)
            load_x(0 * CHUNK, 0)
            sp.dma_start(w[:, :, :], wts.rearrange("n i o -> i n o")).then_inc(w_in, 16)
            sp.dma_start(bcol[:, :], bias_cols).then_inc(w_in, 16)
            sp.dma_start(bvc[:, :], bv_cols).then_inc(w_in, 16)
            sp.dma_start(bor[:, :, :], bo_rows).then_inc(w_in, 16)
            load_x(1 * CHUNK, 1)
            load_ctx(0 * CHUNK, 2)
            load_ctx(1 * CHUNK, 3)
            load_masks(0 * CHUNK, 2)
            load_masks(1 * CHUNK, 3)
            sp.dma_start(cT[:, :], centro).then_inc(ffw_in, 16)
            sp.dma_start(lng[:, :], ln_g).then_inc(ffw_in, 16)
            sp.dma_start(lnb[:, :], ln_b).then_inc(ffw_in, 16)
            sp.dma_start(w1raw[:, :, :], w1t.rearrange("e d f -> d e f")).then_inc(ffw_in, 16)
            sp.dma_start(b1raw[:, :, :], b1c).then_inc(ffw_in, 16)
            for e in range(E):
                sp.dma_start(wpack[:, e, F:2 * F].rearrange("p (c d) -> p c d", c=FC),
                             w2t[e, :, :].rearrange("(c p) d -> p c d", p=P)).then_inc(ffw_in, 16)
                sp.dma_start(wpack[:, e, 2 * F + FC:WCOLS], b2[e:e + 1, :].to_broadcast([P, D])).then_inc(ffw_in, 16)

            with sp.Fori(0, ITERS - 1) as it:
                for k in range(2):
                    row = ((it + 1) * 2 + k) * CHUNK
                    sp.wait_ge(xn_ok, it * PH + (k + 3))
                    load_x(row, k)
                    sp.wait_ge(p_mm, written(it, k + 2, "C"))
                    load_ctx(row, k + 2)
                    sp.wait_ge(madd_ok, it * 2 + (k + 1))
                    load_masks(row, k + 2)

            sp.wait_ge(ffw_in, 16 * (5 + 2 * E))
            sp.wait_ge(scaled, 1)
            sp.wait_ge(scattered, 16 * NT)
            sp.wait_ge(et_ok, 1)

            def load_tile(tile, r):
                row = sp.snap(tile * P)
                expert = sp.value_load(et[0:1, bass.ds(tile, 1)], min_val=0, max_val=E - 1)
                col = sp.snap(expert * WCOLS)
                sp.dma_start(xt[r][:, :], xs_dram[bass.ds(row, P), :]).then_inc(xt_in[r], 16)
                sp.dma_start(wb[r][:, :], wflat[:, bass.ds(col, WCOLS)]).then_inc(wb_in[r], 16)

            def store_and_load(i, last):
                for j in range(FU):
                    sp.wait_ge(y_ok, i * FU + (j + 1 + Y0))
                    sp.dma_start(ys_dram[bass.ts(i * FU + j, P), :], yt[j % 4][:, :]).then_inc(yt_out[j % 4], 16)
                    if not (last and j + 4 >= FU):
                        load_tile(i * FU + (j + 4), j % 4)

            for j in range(4):
                load_tile(j, j)
            with sp.Fori(0, FT // FU - 1) as i:
                store_and_load(i, False)
            store_and_load(FT // FU - 1, True)
            for c in range(NT // 4):
                sp.wait_ge(out_ok, 4 * c + 4)
                sp.dma_start(out[c * CHUNK:(c + 1) * CHUNK, :].rearrange("(u p) d -> p u d", p=P),
                             base[:, 4 * c:4 * c + 4, :]).then_inc(out_done, 16)
            sp.wait_ge(out_done, 16 * (NT // 4))

        @block.tensor
        def _(pe):
            def item(it, k, name):
                par, bk = k % 2, bankP[pbank(k, name)]
                if place(k, name) > 1 or k > 0:
                    pe.wait_ge(p_read[pbank(k, name)], earlier_read(it, k, name))
                self_attn = k % PH < 2
                src = xnT if self_attn else cxT
                if name == "T":
                    pe.wait_ge(xn_ok, it * PH + (k + 1))
                    for u in range(UNITS):
                        last = nc.tensor.transpose(bk[:, u * P:(u + 1) * P], xn[:, u, :], ident)
                elif name == "C":
                    pe.wait_ge(c_in[par], it * 16 + 16)
                    for u in range(UNITS):
                        last = nc.tensor.transpose(bk[:, u * P:(u + 1) * P], cin[par][:, u, :], ident)
                elif name[0] == "S":
                    part, g = "KQ".index(name[1]), int(name[2])
                    if g == 0:
                        pe.wait_ge(hi_ok, it * (PH * 2) + (k * 2 + part + 1))
                        pe.wait_ge(lo_ok, it * (PH * 2) + (k * 2 + part + 1))
                    for hl, halves in enumerate((phi[part], plo[part])):
                        last = nc.tensor.matmul(bk[0:STK, :], sel16[:, part, hl, g, :], halves[:, :], start=hl == 0, stop=hl == 1)
                elif name in ("V0", "V1"):
                    for j in range(4):
                        seq = 4 * int(name[1]) + j
                        last = nc.tensor.matmul(bk[:, j * D:(j + 1) * D], src[:, seq, :, :].rearrange("p a s -> p (a s)"),
                                                w[:, WV if self_attn else XV, :], start=True, stop=True)
                else:
                    if name == "K":
                        for n in ("T",) if self_attn else ("T", "C"):
                            pe.wait_ge(p_read[pbank(k, n)], read_out(it, k, n))
                    wi = {"Q": WQ, "Qr": WQR, "K": WK, "Kr": WKR}[name] if self_attn else {"Q": XQ, "K": XK}[name]
                    last = nc.tensor.matmul(bk[:, :].rearrange("p (b s) -> p b s", b=SEQS), w[:, wi, :], (xnT if name[0] == "Q" else src)[:, :, 0, :], start=True, stop=True)
                last.then_inc(p_mm, 1)

            UB = PH * UNITS

            def scores(it, k, u):
                par = k % 2
                if u == 0 and k % PH > 1:
                    pe.wait_ge(madd_ok, it * 2 + (k - 1))
                if u == 0:
                    pe.wait_ge(kbd_ok, it * (PH * GH) + (k + 1) * GH)
                    for name in ("SQ2", "SQ3"):
                        pe.wait_ge(p_read[pbank(k, name)], read_out(it, k, name))
                for h in range(2):
                    if k > 0 or u > 0:
                        pe.wait_ge(mx_ok, it * 2 * UB + (2 * (k * UNITS + u) - 1 + h))
                    cross = k % PH > 1
                    if cross:
                        nc.tensor.matmul(bankA[h][:, :], idb[:, :], madd[par][:, 0, u, :].unsqueeze(1).broadcast_to([P, 8, S]),
                                         start=True, stop=False, skip_group_check=True)
                    for gl in range(2):
                        g = 2 * h + gl
                        for b in range(2):
                            tok = slice(u * P + b * S, u * P + (b + 1) * S)
                            last = nc.tensor.matmul(
                                bankA[h][b * S:(b + 1) * S, gl * 256:(gl + 1) * 256], qs[par][:, g, tok],
                                kbd[par][:, g, 2 * u + b, :, :].rearrange("p s t -> p (s t)"), start=not cross, stop=True, skip_group_check=cross)
                    last.then_inc(a_mm, 1)

            def scores_t(it, k, u, b):
                par = k % 2
                if b == 0:
                    pe.wait_ge(mx_ok, it * 2 * UB + 2 * (k * UNITS + u + 1))
                pe.wait_ge(exp_ok, it * 2 * UB + (2 * (k * UNITS + u) + b - 1 + EXP0))
                tok = slice(u * P + b * S, u * P + (b + 1) * S)
                for pr in range(PAIRS):
                    for t in range(2):
                        nc.tensor.matmul(bankB[b][t * S:(t + 1) * S, pr * S:(pr + 1) * S],
                                         mx[u % 2][:, 2 * pr + t:2 * pr + t + 1].broadcast_to([P, S]),
                                         negid[:, b * S:(b + 1) * S], start=(pr == 0), stop=False, skip_group_check=True)
                for pr in range(PAIRS):
                    g, s0 = pr // 2, 2 * (pr % 2)
                    last = nc.tensor.matmul(bankB[b][:, pr * S:(pr + 1) * S], kbd[par][:, g, 2 * u + b, s0:s0 + 2, :].rearrange("p s t -> p (s t)"),
                                            qs[par][:, g, tok], start=False, stop=(pr == PAIRS - 1), skip_group_check=True)
                if k % PH > 1:
                    last = nc.tensor.matmul(bankB[b][:, :], dupid[b][:, :, :].rearrange("p a s -> p (a s)"),
                                            madd[par][:, 1, u, :].unsqueeze(1).broadcast_to([P, PAIRS, S]),
                                            start=False, stop=True, skip_group_check=True)
                last.then_inc(b_mm, 1)

            def attend(it, k, u):
                par = k % 2
                if u == 0:
                    for name in ("V0", "V1"):
                        pe.wait_ge(p_read[pbank(k, name)], read_out(it, k, name))
                pe.wait_ge(on_ok, it * UB + (k * UNITS + u + START))
                for b in range(2):
                    pe.wait_ge(exp_ok, it * 2 * UB + (2 * (k * UNITS + u) + b + 1 + EXP0))
                    for pr in range(PAIRS):
                        last = nc.tensor.matmul(bankO[b * S:(b + 1) * S, pr * 18:(pr + 1) * 18],
                                                prob[(2 * u + b) % 4][:, pr * S:(pr + 1) * S],
                                                v9[par][:, 2 * u + b, pr, :, :].rearrange("p a d -> p (a d)"), start=True, stop=True)
                    last.then_inc(pv_mm, 1)

            def out_transpose(it, k, u):
                pe.wait_ge(on_ok, it * UB + (k * UNITS + u + 1 + START))
                pe.wait_ge(res_ok, it * UB + (k * UNITS + u + START))
                nc.tensor.transpose(bankY[:, 0:P], on[:, :, :].rearrange("p h d -> p (h d)"), ident).then_inc(ot_mm, 1)

            def out_project(it, k, u):
                pe.wait_ge(ot_ok, it * UB + (k * UNITS + u + 1))
                nc.tensor.matmul(bankY[:, P:2 * P], onT[:, :], w[:, WO if k % PH < 2 else XO, :],
                                 start=True, stop=True).then_inc(wo_mm, 1)

            pe.sem_inc(pv_mm, PV0)
            for s in (ot_mm, b_mm, xlT_mm, h_mm):
                pe.sem_inc(s, START)
            pe.sem_inc(aff_mm, AFM0)
            pe.sem_inc(y_mm, Y0)
            pe.wait_ge(w_in, 80)
            pe.wait_ge(setup_dve, 8)
            for a in range(2):
                nc.tensor.matmul(bankY[:, a * P:(a + 1) * P], bvc[:, a:a + 1].broadcast_to([P, P]), w[:, WO if a == 0 else XO, :],
                                 start=True, stop=False)
                last = nc.tensor.matmul(bankY[:, a * P:(a + 1) * P], ones[0:1, :], bor[0:1, a, :], start=False, stop=True)
            last.then_inc(bo_mm, 1)
            for name in items(0):
                item(0, 0, name)
            scores(0, 0, 0)
            pe.wait_ge(bo_done, 1)

            def body(it, last):
                for k in range(PH):
                    for u in range(UNITS):
                        first, final = k == 0 and u == 0, k == PH - 1 and u == UNITS - 1
                        pk, pu = (k, u - 1) if u else (k - 1, UNITS - 1)
                        scores_t(it, k, u, 0)
                        if not first:
                            out_transpose(it, pk, pu)
                        scores_t(it, k, u, 1)
                        if not first:
                            out_project(it, pk, pu)
                        ahead = not (last and k == PH - 1)
                        for name in step_items(k + 1, u, 0) if ahead else ():
                            item(it, k + 1, name)
                        if not (last and final):
                            scores(it, k + (u + 1) // UNITS, (u + 1) % UNITS)
                        attend(it, k, u)
                        for name in step_items(k + 1, u, 1) if ahead else ():
                            item(it, k + 1, name)
                out_transpose(it, PH - 1, UNITS - 1)
                out_project(it, PH - 1, UNITS - 1)

            with pe.Fori(0, ITERS - 1) as it:
                body(it, False)
            body(ITERS - 1, True)

            pe.wait_ge(ffw_in, 16 * (5 + 2 * E))
            pe.wait_ge(res_ok, NT * 2 + START)
            for e in range(E):
                for c in range(FC):
                    last = nc.tensor.matmul(bankY[:, e * FC + c:e * FC + c + 1], w1raw[:, e, c * P:(c + 1) * P], lnb[:, e:e + 1],
                                            start=True, stop=True)
            last.then_inc(b1_mm, 1)
            def affinity(i, j):
                pe.wait_ge(xlT_ok, i * 4 + (j + 1 + XLT0))
                pe.wait_ge(aff_ok, i * 4 + (j - 1 + AFF0))
                nc.tensor.matmul(bankB[j % 2][:, 0:E], xlT[j][:, :], cT[:, :], start=True, stop=True).then_inc(aff_mm, 1)

            with pe.Fori(0, NT // 4) as i:
                for j in range(4):
                    pe.wait_ge(xl_ok, i * 4 + (j + 1))
                    pe.wait_ge(xlT_ok, i * 4 + (j - 1 + XLT0))
                    nc.tensor.transpose(bankA[j % 2][:, 0:P], xl[j][:, :], ident).then_inc(xlT_mm, 1)
                    if j > 0:
                        affinity(i, j - 1)
                affinity(i, 3)
            pe.wait_ge(oh_ok, 1)
            nc.tensor.matmul(bankP[0][:, 0:E * NT], tri, oh[:, :, :].rearrange("p e t -> p (e t)"), start=True, stop=True)
            nc.tensor.matmul(bankP[1][:, 0:E * NT], ones[:, :], oh[:, :, :].rearrange("p e t -> p (e t)"),
                             start=True, stop=True).then_inc(rank_mm, 1)

            pe.wait_ge(rank_ok, 1)

            def up_t(i, j):
                pe.wait_ge(xt_in[j % 4], i * (FU // 4 * 16) + (j // 4 + 1) * 16)
                pe.wait_ge(xtT_ok, i * FU + (j - 1 + XT0))
                nc.tensor.transpose(bankA[j % 2][:, 0:P], xt[j % 4][:, :], ident).then_inc(xtT_mm, 1)

            def up(i, j):
                pe.wait_ge(xtT_ok, i * FU + (j + 1 + XT0))
                pe.wait_ge(wb_in[j % 4], i * (FU // 4 * 16) + (j // 4 + 1) * 16)
                pe.wait_ge(relu_act, i * FU + (j - 1 + RELU0))
                pe.wait_ge(relu_dve, i * FU + (j - 1 + Y0))
                for c in range(FC):
                    dst = (bankB, bankP)[c // 2][j % 2]
                    last = nc.tensor.matmul(dst[:, (c % 2) * P:(c % 2 + 1) * P], wb[j % 4][:, c * P:(c + 1) * P], xtT[j % 2][:, :],
                                            start=True, stop=True)
                last.then_inc(h_mm, 1)

            def down(i, j):
                pe.wait_ge(relu_act, i * FU + (j + 1 + RELU0))
                pe.wait_ge(relu_dve, i * FU + (j + 1 + Y0))
                pe.wait_ge(y_ok, i * FU + (j - 1 + Y0))
                dst = (bankO, bankY)[j % 2]
                for c in range(FC):
                    last = nc.tensor.matmul(dst[:, 0:D], hT[j % 2][:, c, :], wb[j % 4][:, F + c * P:F + (c + 1) * P],
                                            start=(c == 0), stop=(c == FC - 1))
                last.then_inc(y_mm, 1)

            with pe.Fori(0, FT // FU) as i:
                up_t(i, 0)
                for j in range(FU):
                    if j + 1 < FU:
                        up_t(i, j + 1)
                    up(i, j)
                    if j > 0:
                        down(i, j - 1)
                down(i, FU - 1)

        @block.scalar
        def _(act):
            UB = PH * UNITS
            act.sem_inc(xhat_ok, START)
            act.sem_inc(exp_ok, EXP0)
            act.sem_inc(xlT_ok, XLT0)
            act.sem_inc(xtT_ok, XT0)
            act.sem_inc(relu_act, RELU0)
            act.wait_ge(w_in, 80)

            def copy_rows(it, k, name, dst):
                act.wait_ge(p_mm, written(it, k, name))
                nc.scalar.activation(dst[:, :, :, :], bankP[pbank(k, name)][:, :].rearrange("p (b s) -> p b s", b=SEQS)
                                     .unsqueeze(2).broadcast_to([P, SEQS, 2, S]), ACT.Copy).then_inc(p_read[pbank(k, name)], 1)

            def high(it, k, part):
                name = "KQ"[part]
                if k % PH < 2:
                    act.wait_ge(rope_ok, it * 4 + (2 * (k if k < PH else 2) + part + 1))
                    nc.scalar.activation(phi[part][:, :], p32[part][:, :], ACT.Copy).then_inc(hi_ok, 1)
                else:
                    bk = bankP[pbank(k, name)]
                    bias = bcol[:, 5 - part:6 - part]
                    act.wait_ge(p_mm, written(it, k, name))
                    nc.scalar.activation(phi[part][:, :], bk[:, :], ACT.Identity, bias=bias).then_inc(hi_ok, 1)
                    act.wait_ge(lo_ok, it * (PH * 2) + (k * 2 - 1 + part))
                    nc.scalar.activation(p32[part][:, :], bk[:, :], ACT.Identity, bias=bias).then_inc(p_read[pbank(k, name)], 1)

            def values(it, k, name):
                bk, j = bankP[pbank(k, name)], int(name[1])
                if k > 0:
                    act.wait_ge(pv_mm, it * 2 * UB + ((k - 1) * 2 * UNITS + PV0))
                act.wait_ge(p_mm, written(it, k, name))
                src = bk[:, :].rearrange("p (b r t d) -> p b r t d", b=4, r=PAIRS, t=2)
                for t in range(2):
                    half = slice(t * S, (t + 1) * S)
                    ins = nc.scalar.activation(v9[k % 2][half, 4 * j:4 * j + 4, :, t, 0:HD], src[half, :, :, t, :], ACT.Copy)
                ins.then_inc(p_read[pbank(k, name)], 1)

            def stack(it, k, name):
                bk, g = bankP[pbank(k, name)], int(name[2])
                act.wait_ge(p_mm, written(it, k, name))
                nc.scalar.activation((ks if name[1] == "K" else qs[k % 2])[:, g, :], bk[0:STK, :], ACT.Copy)\
                    .then_inc(p_read[pbank(k, name)], 1)

            def exps(it, k, u, b):
                act.wait_ge(b_mm, it * 2 * UB + (2 * (k * UNITS + u) + b + 1 + START))
                act.wait_ge(pv_mm, it * 2 * UB + (2 * (k * UNITS + u) + b - 3 + PV0))
                nc.scalar.activation(prob[(2 * u + b) % 4][:, :], bankB[b][:, :], ACT.Exp, scale=SCALE).then_inc(exp_ok, 1)

            def copy_out_t(it, k, u):
                act.wait_ge(ot_mm, it * UB + (k * UNITS + u + 1 + START))
                nc.scalar.activation(onT[:, :], bankY[:, 0:P], ACT.Copy).then_inc(ot_ok, 1)

            def prepare(it, k, names):
                for name in names:
                    if name == "T":
                        copy_rows(it, k, name, xnT)
                    elif name == "C":
                        copy_rows(it, k, name, cxT)
                    elif name in ("K", "Q"):
                        high(it, k, 0 if name == "K" else 1)
                    elif name[0] == "S":
                        stack(it, k, name)
                    elif name in ("V0", "V1"):
                        values(it, k, name)

            act.wait_ge(bo_mm, 1)
            nc.scalar.activation(bo_eff[:, :, :].rearrange("p a d -> p (a d)"), bankY[:, 0:2 * P], ACT.Copy).then_inc(bo_done, 1)
            act.wait_ge(v9_ok, 1)
            prepare(0, 0, items(0))

            def body(it, last):
                for k in range(PH):
                    for u in range(UNITS):
                        first = k == 0 and u == 0
                        ahead = not (last and k == PH - 1)
                        exps(it, k, u, 0)
                        if ahead and u == 2:
                            prepare(it, k + 1, ["K"])
                        if not first:
                            copy_out_t(it, *((k, u - 1) if u else (k - 1, UNITS - 1)))
                        exps(it, k, u, 1)
                        if ahead:
                            prepare(it, k + 1, [n for after in range(2) for n in step_items(k + 1, u, after) if n != "K"])
                copy_out_t(it, PH - 1, UNITS - 1)

            with act.Fori(0, ITERS - 1) as it:
                body(it, False)
            body(ITERS - 1, True)

            act.wait_ge(r_ok, 1)
            with act.Fori(0, NT // 4) as i:
                for j in range(4):
                    act.wait_ge(xlT_mm, i * 4 + (j + 1 + START))
                    act.wait_ge(aff_mm, i * 4 + (j - 3 + AFM0))
                    nc.scalar.activation(xlT[j][:, :], bankA[j % 2][:, 0:P], ACT.Copy).then_inc(xlT_ok, 1)
                    act.wait_ge(xl_ok, i * 4 + (j + 1))
                    nc.scalar.activation(xhat[:, bass.ds(i * 4 + j, 1), :].rearrange("p a d -> p (a d)"), xl[j][:, :], ACT.Copy,
                                         scale=r2[:, bass.ds(i * 4 + j, 1)]).then_inc(xhat_ok, 1)
            act.wait_ge(amax_ok, 1)
            nc.scalar.activation(alpha[:, :], amax[:, :], ACT.Exp, scale=-1.0).then_inc(sig_ok, 1)

            with act.Fori(0, FT // FU) as i:
                for j in range(FU):
                    act.wait_ge(xtT_mm, i * FU + (j + 1))
                    act.wait_ge(h_mm, i * FU + (max(j - 1, 0) + START))
                    nc.scalar.activation(xtT[j % 2][:, :], bankA[j % 2][:, 0:P], ACT.Copy).then_inc(xtT_ok, 1)
                    act.wait_ge(h_mm, i * FU + (j + 1 + START))
                    act.wait_ge(y_mm, i * FU + (j - 1 + Y0))
                    for c in range(2):
                        ins = nc.scalar.activation(hT[j % 2][:, c, :], bankB[j % 2][:, c * P:(c + 1) * P], ACT.Relu,
                                                   bias=wb[j % 4][:, 2 * F + c:2 * F + c + 1])
                    ins.then_inc(relu_act, 1)

        @block.vector
        def _(dve):
            UB = PH * UNITS
            for s in [on_ok, res_ok] + yt_out:
                dve.sem_inc(s, START)
            for i in range(2):
                nc.vector.memset(v9[i][:, :, :, :, :], 0.0).then_inc(v9_zero, 1)
            dve.wait_ge(v9_zero, 2)
            for i in range(2):
                for t in range(2):
                    ins = nc.vector.memset(v9[i][t * S:(t + 1) * S, :, :, t, HD], 1.0)
            ins.then_inc(v9_ok, 1)
            nc.vector.memset(sel16[:, :, :, :, :], 0.0).then_inc(sel_zero, 1)
            nc.vector.memset(ones[:, :], 1.0).then_inc(setup_dve, 1)
            dve.wait_ge(w_in, 80)
            nc.vector.tensor_scalar(negid[:, :], ident, -1.0, None, ALU.mult).then_inc(setup_dve, 1)
            nc.vector.tensor_copy(idb[:, :], ident).then_inc(setup_dve, 1)
            for b in range(2):
                for t in range(2):
                    nc.vector.tensor_copy(dupid[b][:, t, :], cst[:, C_ID + b * S:C_ID + (b + 1) * S]).then_inc(setup_dve, 1)

            dve.wait_ge(sel_zero, 1)
            for part, blocks in enumerate((((0, 2), (1,)), ((0, 1), (2,)))):
                for hl in range(2):
                    for blk in blocks[hl]:
                        ins = nc.vector.tensor_copy(sel16[:, part, hl, :, 32 * blk:32 * blk + 32],
                                                    ident.rearrange("p (g r) -> p g r", g=GROUPS))
            ins.then_inc(setup_dve, 1)

            def rows(k, u):
                return (xin if k % PH < 2 else x1)[k % 2][:, u, :]

            def row_stats(it, k, u):
                if k % PH < 2:
                    if u == 0:
                        dve.wait_ge(x_in[k % 2], it * 16 + (16 if k < PH else 32))
                else:
                    dve.wait_ge(res_ok, it * UB + ((k - 2) * UNITS + u + 1 + START))
                ins = nc.vector.bn_stats(stats[:, u, :], rows(k, u))
                if u == UNITS - 1:
                    ins.then_inc(ln_own, 1)

            def moments(it, k):
                dve.wait_ge(ln_own, it * PH + (k + 1))
                nc.vector.memset(scratch[:, :], 0.0).then_inc(spare, 1)
                for u in range(UNITS):
                    ins = nc.vector.bn_aggr(mv[:, u, :], stats[:, u, :])
                ins.then_inc(ln_stats, 1)

            def norm(it, k):
                if k > 0:
                    dve.wait_ge(p_mm, written(it, k - 1, "T"))
                dve.wait_ge(rstd_ok, it * PH + (k + 1))
                for u in range(UNITS):
                    ins = nc.vector.tensor_scalar(xn[:, u, :], rows(k, u), mv[:, u, 0:1], rstd[:, u:u + 1], ALU.subtract, ALU.mult)
                ins.then_inc(xn_ok, 1)

            def rotate(it, k, name):
                part = 0 if name[0] == "K" else 1
                if name in ("K", "Q") and k > 0:
                    dve.wait_ge(lo_ok, it * (PH * 2) + (2 * k - 1 + part))
                dve.wait_ge(p_mm, written(it, k, name))
                rot = len(name) > 1
                bi = {"Q": 0, "Qr": 1, "K": 2, "Kr": 3}[name]
                col = C_SIN if rot else C_COS
                nc.vector.scalar_tensor_tensor(
                    (t_sin if rot else p32)[part][:, :].rearrange("p (b s) -> p b s", b=SEQS),
                    bankP[pbank(k, name)][:, :].rearrange("p (b s) -> p b s", b=SEQS), bcol[:, bi:bi + 1],
                    cst[:, col:col + S].unsqueeze(1).broadcast_to([P, SEQS, S]), ALU.add, ALU.mult).then_inc(p_read[pbank(k, name)], 1)

            def mask_terms(it, k):
                dve.wait_ge(m_in[k % 2], it * 32 + 32)
                dve.wait_ge(b_mm, it * 2 * UB + ((k - 1) * 2 * UNITS + START))
                nc.vector.tensor_scalar(madd[k % 2][:, :, :, :], mraw[k % 2][:, :, :, :], 0.0, MASKED, ALU.is_equal, ALU.mult)\
                    .then_inc(madd_ok, 1)

            def mask_keys(it, k):
                for name in ("SK2", "SK3"):
                    dve.wait_ge(p_read[pbank(k, name)], read_out(it, k, name))
                if k > 0:
                    dve.wait_ge(b_mm, it * 2 * UB + ((k - 1) * 2 * UNITS + START))
                for s in range(GH):
                    nc.vector.tensor_scalar(kbd[k % 2][:, :, :, s, :], ks[:, :, :].rearrange("p g (b t) -> p g b t", b=SEQS), cst[0:STK, C_MASK + s:C_MASK + s + 1],
                                            None, ALU.mult).then_inc(kbd_ok, 1)

            def maxima(it, k, u):
                if k > 0 or u > 0:
                    dve.wait_ge(b_mm, it * 2 * UB + (2 * (k * UNITS + u) - 2 + START))
                for h in range(2):
                    dve.wait_ge(a_mm, it * 2 * UB + (2 * (k * UNITS + u) + h + 1))
                    nc.vector.tensor_reduce(mx[u % 2][:, 8 * h:8 * h + 8], bankA[h][:, :].rearrange("p (h t) -> p h t", t=S),
                                            AX.X, ALU.max).then_inc(mx_ok, 1)

            def normalise(it, k, u):
                dve.wait_ge(pv_mm, it * 2 * UB + (2 * (k * UNITS + u) + 2 + PV0))
                o9 = bankO[:, 0:H * 9].rearrange("p (h d) -> p h d", h=H)
                nc.vector.reciprocal(rden[:, :], o9[:, :, HD]).then_inc(rden_ok, 1)
                dve.wait_ge(rden_ok, it * UB + (k * UNITS + u + 1))
                dve.wait_ge(ot_mm, it * UB + (k * UNITS + u + START))
                nc.vector.tensor_tensor(on[:, :, :], o9[:, :, 0:HD], rden[:, :].unsqueeze(2).broadcast_to([P, H, HD]),
                                        ALU.mult).then_inc(on_ok, 1)

            def residual(it, k, u):
                dve.wait_ge(wo_mm, it * UB + (k * UNITS + u + 1))
                if u == 0:
                    dve.wait_ge(xb_ok, it * PH + (k + 1))
                if k % PH < 2:
                    dst = x1[k % 2][:, u, :]
                else:
                    dst = x2[:, bass.ds(it * (2 * UNITS) + ((k % 2) * UNITS + u), 1), :].rearrange("p a d -> p (a d)")
                nc.vector.tensor_tensor(dst, bankY[:, P:2 * P], xb[k % 2][:, u, :], ALU.add).then_inc(res_ok, 1)

            for u in range(UNITS):
                row_stats(0, 0, u)
            moments(0, 0)
            norm(0, 0)
            for name in ("K", "Kr", "Q", "Qr"):
                rotate(0, 0, name)
            mask_keys(0, 0)
            maxima(0, 0, 0)

            def body(it, last):
                for k in range(PH):
                    for u in range(UNITS):
                        ahead = not (last and k == PH - 1)
                        if k or u:
                            pk, pu = (k, u - 1) if u else (k - 1, UNITS - 1)
                            residual(it, pk, pu)
                            if pk % PH < 2:
                                row_stats(it, pk + 2, pu)
                        if ahead:
                            if u == 0:
                                if (k + 1) % PH < 2:
                                    for v in range(UNITS):
                                        row_stats(it, k + 1, v)
                                moments(it, k + 1)
                            if u == 1 and (k + 1) % PH > 1:
                                mask_terms(it, k + 1)
                            if u == 2 and (k + 1) % PH < 2:
                                rotate(it, k + 1, "Q")
                                rotate(it, k + 1, "Qr")
                            if u == UNITS - 1:
                                mask_keys(it, k + 1)
                        if not (last and k == PH - 1 and u == UNITS - 1):
                            maxima(it, k + (u + 1) // UNITS, (u + 1) % UNITS)
                        normalise(it, k, u)
                        if ahead:
                            if u == 0:
                                norm(it, k + 1)
                            if u == 1 and (k + 1) % PH < 2:
                                rotate(it, k + 1, "K")
                                rotate(it, k + 1, "Kr")
                residual(it, PH - 1, UNITS - 1)

            with dve.Fori(0, ITERS - 1) as it:
                body(it, False)
            body(ITERS - 1, True)

            dve.wait_ge(res_ok, 2 * NT + START)
            for t in range(NT):
                ins = nc.vector.bn_stats(stat3[:, t, :], x2[:, t, :])
            ins.then_inc(mv3_own, 1)
            dve.wait_ge(mv3_own, 1)
            for t in range(NT):
                ins = nc.vector.bn_aggr(mv3[:, t, :], stat3[:, t, :])
            ins.then_inc(mv3_ok, 1)
            dve.wait_ge(b1_mm, 1)
            nc.vector.tensor_tensor(wpack[:, :, 2 * F:2 * F + FC], bankY[:, 0:E * FC].rearrange("p (e c) -> p e c", e=E),
                                    b1raw[:, :, :], ALU.add).then_inc(b1_ok, 1)
            dve.sem_inc(aff_ok, AFF0)
            dve.wait_ge(r_ok, 1)
            with dve.Fori(0, NT // 4) as i:
                for j in range(4):
                    one = bass.ds(i * 4 + j, 1)
                    dve.wait_ge(xlT_mm, i * 4 + START)
                    dve.wait_ge(xhat_ok, i * 4 + START)
                    dve.wait_ge(base_ok, i * 4 + START)
                    nc.vector.tensor_scalar(xl[j][:, :], x2[:, one, :].rearrange("p a d -> p (a d)"),
                                            mv3[:, one, 0:1].rearrange("p a d -> p (a d)"), r1[:, one],
                                            ALU.subtract, ALU.mult).then_inc(xl_ok, 1)
                for j in range(4):
                    dve.wait_ge(aff_mm, i * 4 + (j + 1 + AFM0))
                    nc.vector.tensor_copy(aff[:, bass.ds(i * 4 + j, 1), :].rearrange("p a d -> p (a d)"),
                                          bankB[j % 2][:, 0:E]).then_inc(aff_ok, 1)

            step = [0]

            def chained(ins):
                step[0] += 1
                ins.then_inc(route, 1)
                dve.wait_ge(route, step[0])

            dve.wait_ge(aff_ok, NT + AFF0)
            nc.vector.tensor_reduce(amax[:, :], aff[:, :, :], AX.X, ALU.max).then_inc(amax_ok, 1)
            dve.wait_ge(amax_ok, 1)
            chained(nc.vector.tensor_tensor(eq[:, :, :], aff[:, :, :], amax[:, :].unsqueeze(2).broadcast_to([P, NT, E]), ALU.is_ge))
            chained(nc.vector.tensor_tensor(eq[:, :, :], eq[:, :, :], cst[:, C_RANK:C_RANK + E].unsqueeze(1).broadcast_to([P, NT, E]),
                                            ALU.mult))
            chained(nc.vector.tensor_reduce(sel[:, :], eq[:, :, :], AX.X, ALU.max))
            nc.vector.tensor_tensor(oh[:, :, :], sel[:, :].unsqueeze(1).broadcast_to([P, E, NT]),
                                    cst[:, C_RANK:C_RANK + E].unsqueeze(2).broadcast_to([P, E, NT]), ALU.is_equal).then_inc(oh_ok, 1)
            dve.wait_ge(rank_mm, 1)
            nc.vector.tensor_copy(pre[:, :, :].rearrange("p e t -> p (e t)"), bankP[0][:, 0:E * NT])
            chained(nc.vector.tensor_copy(tot[:, :, :].rearrange("p e t -> p (e t)"), bankP[1][:, 0:E * NT]))
            chained(nc.vector.tensor_tensor_scan(inc[:, :, :].rearrange("p e t -> p (e t)"), cst[:, C_SEG:C_SEG + E * NT],
                                                 tot[:, :, :].rearrange("p e t -> p (e t)"), 0.0, ALU.mult, ALU.add))
            chained(nc.vector.tensor_scalar(gt[:, :], cst[:, C_IOTA:C_IOTA + NT], float(P), None, ALU.mult))
            chained(nc.vector.tensor_tensor(gt2[:, :, :], inc[:, :, NT - 1].unsqueeze(2).broadcast_to([P, E, NT]),
                                            gt[:, :].unsqueeze(1).broadcast_to([P, E, NT]), ALU.is_gt))
            chained(nc.vector.tensor_reduce(ntile[:, :], gt2[:, :, :], AX.X, ALU.add))
            chained(nc.vector.tensor_tensor_scan(tinc[:, :], ones[:, 0:E], ntile[:, :], 0.0, ALU.mult, ALU.add))
            chained(nc.vector.tensor_tensor(texc[:, :], tinc[:, :], ntile[:, :], ALU.subtract))
            chained(nc.vector.tensor_tensor(inc[:, :, :], inc[:, :, :], tot[:, :, :], ALU.subtract))
            chained(nc.vector.tensor_tensor(inc[:, :, :], inc[:, :, :], pre[:, :, :], ALU.add))
            chained(nc.vector.scalar_tensor_tensor(inc[:, :, :], texc[:, :].unsqueeze(2).broadcast_to([P, E, NT]), float(P),
                                                   inc[:, :, :], ALU.mult, ALU.add))
            chained(nc.vector.tensor_tensor(inc[:, :, :], inc[:, :, :], oh[:, :, :], ALU.mult))
            chained(nc.vector.tensor_reduce(posf[:, :], inc[:, :, :].rearrange("p e t -> p t e"), AX.X, ALU.add))
            nc.vector.tensor_copy(pos[:, :], posf[:, :]).then_inc(rank_ok, 1)
            chained(nc.vector.tensor_tensor(geq[:, :, :], cst[:, C_IOTA:C_IOTA + FT].unsqueeze(2).broadcast_to([P, FT, E]),
                                            tinc[:, :].unsqueeze(1).broadcast_to([P, FT, E]), ALU.is_ge))
            chained(nc.vector.tensor_reduce(etf[:, :], geq[:, :, :], AX.X, ALU.add))
            chained(nc.vector.tensor_scalar(etf[:, :], etf[:, :], float(E - 1), None, ALU.min))
            nc.vector.tensor_copy(et[:, :], etf[:, :]).then_inc(et_ok, 1)
            dve.wait_ge(sig_ok, 1)
            chained(nc.vector.tensor_scalar(amax[:, :], alpha[:, :], 1.0, None, ALU.add))
            chained(nc.vector.reciprocal(alpha[:, :], amax[:, :]))

            dve.sem_inc(relu_dve, Y0)
            dve.sem_inc(y_ok, Y0)

            def hidden(i, j):
                dve.wait_ge(h_mm, i * FU + (j + 1 + START))
                dve.wait_ge(y_mm, i * FU + (j - 1 + Y0))
                for c in range(2, FC):
                    ins = nc.vector.tensor_scalar(hT[j % 2][:, c, :], bankP[j % 2][:, (c - 2) * P:(c - 1) * P],
                                                  wb[j % 4][:, 2 * F + c:2 * F + c + 1], 0.0, ALU.add, ALU.max)
                ins.then_inc(relu_dve, 1)

            def result(i, j):
                dve.wait_ge(y_mm, i * FU + (j + 1 + Y0))
                dve.wait_ge(yt_out[j % 4], i * (FU // 4 * 16) + (j // 4 * 16 + START))
                nc.vector.tensor_tensor(yt[j % 4][:, :], (bankO, bankY)[j % 2][:, 0:D], wb[j % 4][:, 2 * F + FC:WCOLS],
                                        ALU.add).then_inc(y_ok, 1)

            with dve.Fori(0, FT // FU) as i:
                for j in range(FU):
                    hidden(i, j)
                    if j > 0:
                        result(i, j - 1)
                result(i, FU - 1)

            dve.wait_ge(base_ok, NT + START)
            for t in range(NT):
                dve.wait_ge(yg_in[t // 4], 64)
                nc.vector.scalar_tensor_tensor(base[:, t, :], xhat[:, t, :], alpha[:, t:t + 1], base[:, t, :],
                                               ALU.mult, ALU.add).then_inc(out_ok, 1)

        @block.gpsimd
        def _(pool):
            UB = PH * UNITS
            pool.sem_inc(base_ok, START)
            nc.gpsimd.memset(minus_half[:, :], -0.5)
            nc.gpsimd.memset(eps_col[:, :], EPS)
            nc.gpsimd.memset(xhat[:, 0:8, :], 0.0).then_inc(setup_pool, 1)
            pool.wait_ge(setup_pool, 1)
            for c in range(FT // 8):
                pool.dma_start(xs_dram[c * 8 * P:(c + 1) * 8 * P, :].rearrange("(u p) d -> p u d", p=P),
                               xhat[:, 0:8, :]).then_inc(zeroed, 16)

            def rows(k):
                return (xin if k % PH < 2 else x1)[k % 2]

            def prepare_rows(it, k):
                pool.wait_ge(ln_stats, it * PH + (k + 1))
                if k > 0:
                    pool.wait_ge(xn_ok, it * PH + k)
                nc.gpsimd.tensor_tensor(ve[:, :], mv[:, :, 1], eps_col[:, :], ALU.add).then_inc(rstd_own, 1)
                pool.wait_ge(rstd_own, it * PH + (k + 1))
                nc.gpsimd.tensor_tensor(rstd[:, :], ve[:, :], minus_half[:, 0:UNITS], ALU.pow).then_inc(rstd_ok, 1)
                if k > 0:
                    pool.wait_ge(res_ok, it * UB + ((k - 1) * UNITS + START))
                nc.gpsimd.tensor_tensor(xb[k % 2][:, :, :], rows(k)[:, :, :],
                                        bo_eff[:, (k % PH) // 2, :].unsqueeze(1).broadcast_to([P, UNITS, D]),
                                        ALU.add).then_inc(xb_ok, 1)

            def low(it, k, part):
                name = "KQ"[part]
                if k % PH < 2:
                    pool.wait_ge(p_read[pbank(k, name + "r")], read_out(it, k, name + "r"))
                    if k > 0:
                        pool.wait_ge(lo_ok, it * (PH * 2) + (k * 2 - 1 + part))
                    nc.gpsimd.tensor_tensor(p32[part][:, :], p32[part][:, :], t_sin[part][:, :], ALU.add).then_inc(rope_ok, 1)
                    pool.wait_ge(hi_ok, it * (PH * 2) + (k * 2 + part + 1))
                else:
                    pool.wait_ge(p_read[pbank(k, name)], read_out(it, k, name))
                nc.gpsimd.tensor_tensor(plo[part][:, :], p32[part][:, :], phi[part][:, :], ALU.subtract).then_inc(lo_ok, 1)

            pool.wait_ge(bo_done, 1)
            prepare_rows(0, 0)
            low(0, 0, 0)
            low(0, 0, 1)
            pool.wait_ge(ffw_in, 16 * (5 + 2 * E))
            for e in range(E):
                last = nc.gpsimd.tensor_tensor(wpack[:, e, 0:F], w1raw[:, e, :], lng[:, e:e + 1].broadcast_to([P, F]), ALU.mult)
            last.then_inc(scaled, 1)

            def body(it, last):
                for k in range(1, PH if last else PH + 1):
                    prepare_rows(it, k)
                    low(it, k, 0)
                    low(it, k, 1)

            with pool.Fori(0, ITERS - 1) as it:
                body(it, False)
            body(ITERS - 1, True)

            n = [0]

            def chained(ins):
                n[0] += 1
                ins.then_inc(r_own, 1)
                pool.wait_ge(r_own, n[0])

            pool.wait_ge(mv3_ok, 1)
            chained(nc.gpsimd.tensor_scalar(rtmp[:, :], mv3[:, :, 1], EPS, None, ALU.add))
            chained(nc.gpsimd.tensor_tensor(r1[:, :], rtmp[:, :], minus_half[:, :], ALU.pow))
            chained(nc.gpsimd.tensor_tensor(rtmp[:, :], r1[:, :], r1[:, :], ALU.mult))
            chained(nc.gpsimd.tensor_tensor(rtmp[:, :], rtmp[:, :], mv3[:, :, 1], ALU.mult))
            chained(nc.gpsimd.tensor_scalar(rtmp[:, :], rtmp[:, :], EPS, None, ALU.add))
            pool.wait_ge(zeroed, 16 * (FT // 8))
            nc.gpsimd.tensor_tensor(r2[:, :], rtmp[:, :], minus_half[:, :], ALU.pow).then_inc(r_ok, 1)
            with pool.Fori(0, NT // 4) as i:
                for j in range(4):
                    one = bass.ds(i * 4 + j, 1)
                    pool.wait_ge(xl_ok, i * 4 + (j + 1))
                    nc.gpsimd.tensor_tensor(base[:, one, :].rearrange("p a d -> p (a d)"), xl[j][:, :],
                                            x2[:, one, :].rearrange("p a d -> p (a d)"), ALU.add).then_inc(base_ok, 1)
            pool.wait_ge(xhat_ok, NT + START)
            pool.wait_ge(rank_ok, 1)
            for t in range(NT):
                pool.indirect_dma_start(xs_dram, bass.IndirectOffsetOnAxis(ap=pos[:, t:t + 1], axis=0), xhat[:, t, :], None)\
                    .then_inc(scattered, 16)
            pool.wait_ge(scattered, 16 * NT)
            for r in range(4):
                pool.wait_ge(yt_out[r], FT // 4 * 16 + START)
            for t in range(NT):
                pool.indirect_dma_start(xhat[:, t, :], None, ys_dram, bass.IndirectOffsetOnAxis(ap=pos[:, t:t + 1], axis=0))\
                    .then_inc(yg_in[t // 4], 16)


def kernel(**inputs):
    import numpy as np
    import concourse.bacc as bacc
    from concourse.bass_utils import run_bass_kernel_spmd

    a = {k: np.asarray(v) for k, v in inputs.items()}
    rot = np.arange(D).reshape(H, 2, HD // 2)[:, ::-1].reshape(D)
    wq, wk = a["L0_attn_wq"], a["L0_attn_wk"]
    wts = np.stack([m.T for m in (wq, wq[rot], wk, wk[rot], a["L0_attn_wv"], a["L0_attn_wo"],
                                  a["L0_xattn_qw"], a["L0_xattn_kw"], a["L0_xattn_vw"], a["L0_xattn_ow"])])
    bq, bk = a["L0_attn_bq"], a["L0_attn_bk"]
    bias_cols = np.stack([bq, bq[rot], bk, bk[rot], a["L0_xattn_qb"], a["L0_xattn_kb"]], axis=1)

    consts = np.zeros((P, C_END), np.float32)
    consts[:, C_ID:C_ID + P] = np.eye(P)
    consts[:, C_TRI:C_TRI + P] = np.triu(np.ones((P, P)), 1)
    inv_freq = (1.0 / 10000.0 ** (np.arange(0, HD, 2, dtype=np.float32) / np.float32(HD))).astype(np.float32)
    freqs = np.arange(S, dtype=np.float32)[:, None] * inv_freq[None, :]
    emb = np.concatenate([freqs, freqs], axis=-1)
    sign = np.where(np.arange(HD) < HD // 2, -1.0, 1.0)
    consts[:, C_COS:C_COS + S] = np.tile(np.cos(emb).T, (H, 1))
    consts[:, C_SIN:C_SIN + S] = np.tile((np.sin(emb) * sign).T, (H, 1))
    for s in range(GH):
        consts[:, C_MASK + s] = (np.arange(P) % 32) // HD == s
    consts[:, C_RANK:C_RANK + E] = E - np.arange(E)
    consts[:, C_SEG:C_SEG + E * NT] = np.arange(E * NT) % NT != 0
    consts[:, C_IOTA:C_IOTA + FT] = np.arange(FT)

    arrays = {
        "x": a["x"].reshape(T, D), "ctx": a["ctx_1024"].reshape(T, D),
        "mask_q": a["mask_BxSxS2_if1"].reshape(T, S), "mask_k": a["mask_BxSxS2_if1"].transpose(0, 2, 1).reshape(T, S), "wts": wts, "bias_cols": bias_cols,
        "bv_cols": np.stack([a["L0_attn_bv"], a["L0_xattn_vb"]], axis=1),
        "bo_rows": np.stack([a["L0_attn_bo"], a["L0_xattn_ob"]])[None],
        "consts": consts, "centro": a["L0_ffn_centroids"].T, "ln_g": a["L0_ffn_ln_g"].T, "ln_b": a["L0_ffn_ln_b"].T,
        "w1t": a["L0_ffn_w1"].transpose(0, 2, 1), "w2t": a["L0_ffn_w2"].transpose(0, 2, 1),
        "b1c": a["L0_ffn_b1"].reshape(E, FC, P).transpose(2, 0, 1), "b2": a["L0_ffn_b2"],
    }
    nc = bacc.Bacc("TRN2", target_bir_lowering=False, num_devices=1)
    feed, args = {}, []
    for name, value in arrays.items():
        feed[f"in_{name}"] = np.ascontiguousarray(value)
        args.append(nc.dram_tensor(f"in_{name}", value.shape, mybir.dt.from_np(value.dtype), kind="ExternalInput").ap())
    out = nc.dram_tensor("out", (T, D), mybir.dt.float32, kind="ExternalOutput").ap()
    decoder_layer(nc, *args, out)
    r = run_bass_kernel_spmd(nc, [feed], core_ids=[0])
    return r.results[0]["out"].reshape(B, S, D)
```

```python
import concourse.bass as bass
from concourse import mybir
from contextlib import ExitStack

B, S, D, H = 64, 64, 128, 16
HD = D // H
E, F = 8, 512
P = 128
T = B * S
NT = T // P
CHUNK = 512
UNITS = CHUNK // P
SEQS = CHUNK // S
NCH = T // CHUNK
GROUPS = 4
GH = H // GROUPS
PAIRS = H // 2
STK = 96
FC = F // P
FT = 40
FU = 10
RING = 5
EPS = 1e-5
MASKED = -2.0 ** 40
SCALE = HD ** -0.5
WCOLS = F + F + FC + D

PH = 4
ITERS = NCH // 2

C_ID, C_TRI, C_COS, C_SIN = 0, 128, 256, 320
C_MASK = 384
C_RANK = 388
C_SEG = 396
C_IOTA = C_SEG + E * NT
C_END = C_IOTA + FT

(WQ, WQR, WK, WKR, WV, WO, XQ, XK, XV, XO) = range(10)


def decoder_layer(nc, x, tok_ids, pad_ids, ctx_in, mask_q, mask_k, wts, bias_cols, bv_cols, bo_rows, consts, centro, ln_g, ln_b,
                  w1t, w2t, b1c, b2, out):
    f32, f16, bf16, i32 = mybir.dt.float32, mybir.dt.float16, mybir.dt.bfloat16, mybir.dt.int32
    ALU, ACT, AX = mybir.AluOpType, mybir.ActivationFunctionType, mybir.AxisListType

    es = ExitStack()
    with es:
        def sb(name, shape, dt=f32):
            return es.enter_context(nc.sbuf_tensor(name, shape, dt))

        def sem(name):
            return es.enter_context(nc.semaphore(name))

        xs_dram = nc.dram_tensor("sorted_in", (FT * P, D + 1), f32, kind="Internal").ap()
        ys_dram = nc.dram_tensor("results", (T + FT * P, D), f32, kind="Internal").ap()

        cst = sb("cst", [P, C_END])
        ident = cst[:, C_ID:C_ID + P]
        tri = cst[:, C_TRI:C_TRI + P]
        negid = sb("negid", [P, P], bf16)
        idb = sb("idb", [P, P], bf16)
        dupid = [sb(f"dupid{b}", [P, 2, S], bf16) for b in range(2)]
        sel16 = sb("sel16", [P, 2, 2, GROUPS, STK], f16)
        ones = sb("ones", [P, P])
        minus_half = sb("minus_half", [P, UNITS])
        eps_col = sb("eps_col", [P, UNITS])
        w = sb("w", [P, 10, P])
        bcol = sb("bcol", [P, 6])
        bvc = sb("bvc", [P, 2])
        bor = sb("bor", [1, 2, D])
        bo_eff = sb("bo_eff", [P, 2, D])
        cT = sb("cT", [P, E])
        lng = sb("lng", [P, E])
        lnb = sb("lnb", [P, E])
        w1raw = sb("w1raw", [P, E, F])
        wpack = sb("wpack", [P, E, WCOLS])
        b1raw = sb("b1raw", [P, E, FC])

        xin = [sb(f"xin{i}", [P, UNITS, D]) for i in range(2)]
        cin = [sb(f"cin{i}", [P, UNITS, D]) for i in range(2)]
        x1 = [sb(f"x1_{i}", [P, UNITS, D]) for i in range(2)]
        xb = [sb(f"xb{i}", [P, UNITS, D]) for i in range(2)]
        stack_mem = sb("stack_mem", [P, 3 * GROUPS * CHUNK], f16)
        *qs, ks = [stack_mem[0:STK, i * GROUPS * CHUNK:(i + 1) * GROUPS * CHUNK].rearrange("p (g t) -> p g t", g=GROUPS)
                   for i in range(3)]
        kbd_mem = [sb(f"kbd{i}", [P, GROUPS * GH * CHUNK], f16) for i in range(2)]
        kbd = [m[0:STK, :].rearrange("p (g b s t) -> p g b s t", g=GROUPS, b=SEQS, s=GH) for m in kbd_mem]
        v9 = [sb(f"v9_{i}", [P, SEQS, PAIRS, 2, HD + 1]) for i in range(2)]
        mraw = [sb(f"mraw{i}", [P, 2, UNITS, S], i32) for i in range(2)]
        madd = [sb(f"madd{i}", [P, 2, UNITS, S], bf16) for i in range(2)]
        stats = sb("stats", [P, UNITS, 6])
        mv = sb("mv", [P, UNITS, 2])
        ve = sb("ve", [P, UNITS])
        scratch = sb("scratch", [P, 3])
        spare_pool = sb("spare_pool", [P, FU])
        rstd = sb("rstd", [P, UNITS])
        xn = sb("xn", [P, UNITS, D])
        xnT = sb("xnT", [P, SEQS, 2, S])
        cxT = sb("cxT", [P, SEQS, 2, S])
        t_sin = [sb(f"t_sin{i}", [P, CHUNK]) for i in range(2)]
        p32 = [sb(f"p32_{i}", [P, CHUNK]) for i in range(2)]
        phi = [sb(f"phi{i}", [P, CHUNK], f16) for i in range(2)]
        plo = [sb(f"plo{i}", [P, CHUNK], f16) for i in range(2)]
        mx = [sb(f"mx{i}", [P, H], bf16) for i in range(2)]
        prob = [sb(f"prob{i}", [P, PAIRS * S]) for i in range(4)]
        rden = sb("rden", [P, H])
        on = sb("on", [P, H, HD])
        onT = sb("onT", [P, P])
        late = [stack_mem[:, :].bitcast(f32), kbd_mem[1][:, 2 * WCOLS:].bitcast(f32),
                w1raw[:, :, :].rearrange("p e f -> p (e f)")]

        def late_sb(i, *dims):
            size = 1
            for d in dims:
                size *= d
            got, late[i] = late[i][:, 0:size], late[i][:, size:]
            return got if len(dims) == 1 else got.rearrange("p (a b) -> p a b", a=dims[0])

        x2 = sb("x2", [P, NT, D])
        pads = sb("pads", [P, FT])
        toks = sb("toks", [P, NT])
        xhat = sb("xhat", [P, NT, D + 1])
        stat3 = sb("stat3", [P, UNITS, 6])
        mv3 = sb("mv3", [P, UNITS, 2])
        r1 = sb("r1", [P, UNITS])
        r2 = sb("r2", [P, UNITS])
        rtmp = sb("rtmp", [P, UNITS])
        xl = late_sb(2, UNITS, D)
        xlT = late_sb(2, UNITS, P)
        aff = late_sb(2, NT, E)
        amax = late_sb(0, NT)
        alpha = late_sb(0, NT)
        eq = late_sb(1, NT, E)
        sel = late_sb(0, NT)
        oh = late_sb(1, E, NT)
        pre = late_sb(1, E, NT)
        tot = late_sb(1, E, NT)
        inc = late_sb(1, E, NT)
        gt = late_sb(0, NT)
        gt2 = late_sb(1, E, NT)
        ntile = sb("ntile", [P, E])
        tinc = sb("tinc", [P, E])
        texc = sb("texc", [P, E])
        posf = late_sb(0, NT)
        pos = sb("pos", [P, NT], i32)
        geq = late_sb(1, FT, E)
        etf = late_sb(0, FT)
        et = sb("et", [P, FT], i32)
        wb = [kbd_mem[i // 3][:, (i % 3) * 2 * WCOLS:(i % 3 + 1) * 2 * WCOLS].bitcast(f32) for i in range(4)] + [late_sb(2, WCOLS)]
        xt = [late_sb(0, D + 1) for i in range(RING)]
        xtT = [late_sb(1, P) for i in range(2)]
        hT = [late_sb(i, FC, P) for i in range(2)]
        yt = [late_sb(2, D + 1) for i in range(RING)]

        bank = [es.enter_context(nc.psum_tensor(f"bank{i}", [P, 512], f32)) for i in range(8)]
        bankA, bankB, bankO, bankY, bankP = bank[0:2], bank[2:4], bank[4], bank[5], bank[6:8]

        w_in, x_in, c_in = sem("w_in"), [sem("x_in0"), sem("x_in1")], [sem("c_in0"), sem("c_in1")]
        m_in, madd_ok = [sem("m_in0"), sem("m_in1")], sem("madd_ok")
        ffw_in, w1_in = sem("ffw_in"), sem("w1_in")
        sel_zero = sem("sel_zero")
        setup_dve, setup_pool = sem("setup_dve"), sem("setup_pool")
        v9_zero, v9_ok = sem("v9_zero"), sem("v9_ok")
        bo_mm, bo_done = sem("bo_mm"), sem("bo_done")
        spare, ln_own, ln_stats, rstd_own, rstd_ok = sem("spare"), sem("ln_own"), sem("ln_stats"), sem("rstd_own"), sem("rstd_ok")
        xn_ok, xb_ok = sem("xn_ok"), sem("xb_ok")
        p_mm, p_read = sem("p_mm"), [sem("p_read0"), sem("p_read1")]
        rope_ok, hi_ok, lo_ok = sem("rope_ok"), sem("hi_ok"), sem("lo_ok")
        kbd_ok = sem("kbd_ok")
        a_mm, mx_ok, b_mm, exp_ok, pv_mm = sem("a_mm"), sem("mx_ok"), sem("b_mm"), sem("exp_ok"), sem("pv_mm")
        rden_ok, on_ok, ot_mm, ot_ok, wo_mm, res_ok = (sem("rden_ok"), sem("on_ok"), sem("ot_mm"), sem("ot_ok"),
                                                       sem("wo_mm"), sem("res_ok"))

        b1_mm, b1_ok = sem("b1_mm"), sem("b1_ok")
        mv3_own, mv3_ok, r_own, r_ok = sem("mv3_own"), sem("mv3_ok"), sem("r_own"), sem("r_ok")
        xl_ok = sem("xl_ok")
        xhat_ok, base_ok = sem("xhat_ok"), sem("base_ok")
        route, amax_ok, sig_ok, oh_ok, rank_mm, rank_ok, et_ok = (sem("route"), sem("amax_ok"), sem("sig_ok"), sem("oh_ok"),
                                                                  sem("rank_mm"), sem("rank_ok"), sem("et_ok"))
        zeroed, scattered, scaled = sem("zeroed"), sem("scattered"), sem("scaled")
        wb_in = [sem(f"wb_in{r}") for r in range(RING)]
        xt_in = [sem(f"xt_in{r}") for r in range(RING)]
        yt_out = [sem(f"yt_out{r}") for r in range(RING)]
        xtT_mm, xtT_ok, h_mm, relu_act, relu_dve, y_mm, y_ok = (sem("xtT_mm"), sem("xtT_ok"), sem("h_mm"), sem("relu_act"),
                                                                sem("relu_dve"), sem("y_mm"), sem("y_ok"))
        yg_in = [sem(f"yg_in{c}") for c in range(NT // 4)]
        pad_in, tok_in, yt_taken = sem("pad_in"), sem("tok_in"), sem("yt_taken")
        out_ok, out_done = sem("out_ok"), sem("out_done")
        B1_COL = H * (HD + 1)

        wflat = wpack[:, :, :].rearrange("p e c -> p (e c)")

        START = 1
        EXP0, PV0 = 2, 4
        XT0, RELU0, Y0 = 2, 2, 4

        STEPS_SELF = [[[], [], []], [[], ["T"], ["K", "Kr"]], [["Q", "Qr"], [], ["SK0", "SK1", "SK2", "SK3"]],
                      [["SQ0", "SQ1", "SQ2", "SQ3", "L"], [], ["A", "V0"]], [["V1"]]]
        STEPS_CROSS = [[[], [], []], [[], ["C", "T"], ["K"]], [["Q"], [], ["SK0", "SK1", "SK2", "SK3"]],
                       [["SQ0", "SQ1", "SQ2", "SQ3"], [], ["V0"]], [["V1"]]]
        SELF_ITEMS = [n for step in STEPS_SELF for part in step for n in part]
        CROSS_ITEMS = [n for step in STEPS_CROSS for part in step for n in part]

        def items(k):
            return SELF_ITEMS if k % PH < 2 else CROSS_ITEMS

        def step_items(k, u, when):
            return (STEPS_SELF if k % PH < 2 else STEPS_CROSS)[u][when]

        BODY_USES = 2 * len(SELF_ITEMS) + 2 * len(CROSS_ITEMS)

        def finish_place(it, k, name):
            if isinstance(it, int) and it == ITERS - 1:
                return PH, {"L": "T", "A": "K"}[name] if k < PH else {"L": "Kr", "A": "Q"}[name]
            return k + 1, name

        def finished(it, k):
            return it * 2 + (k - 2)

        def place(k, item):
            return sum(len(items(j)) for j in range(k)) + items(k).index(item)

        def pbank(k, item):
            return place(k, item) % 2

        def written(it, k, item):
            return it * BODY_USES + (place(k, item) + 1)

        def earlier_read(it, k, item):
            return it * (BODY_USES // 2) + place(k, item) // 2

        def read_out(it, k, item):
            return it * (BODY_USES // 2) + (place(k, item) // 2 + 1)

        block = es.enter_context(nc.Block())

        @block.sync
        def _(sp):
            def load_x(row, k):
                sp.dma_start(xin[k % 2][:, :, :],
                             x[bass.ds(row, CHUNK), :].rearrange("(u p) d -> p u d", p=P)).then_inc(x_in[k % 2], 16)

            def load_ctx(row, k):
                sp.dma_start(cin[k % 2][:, :, :],
                             ctx_in[bass.ds(row, CHUNK), :].rearrange("(u p) d -> p u d", p=P)).then_inc(c_in[k % 2], 16)

            def load_masks(row, k):
                for side, m in enumerate((mask_q, mask_k)):
                    sp.dma_start(mraw[k % 2][:, side, :, :],
                                 m[bass.ds(row, CHUNK), :].rearrange("(u p) s -> p u s", p=P)).then_inc(m_in[k % 2], 16)

            sp.dma_start(cst[:, :], consts).then_inc(w_in, 16)
            load_x(0 * CHUNK, 0)
            sp.dma_start(w[:, :, :], wts.rearrange("n i o -> i n o")).then_inc(w_in, 16)
            sp.dma_start(bcol[:, :], bias_cols).then_inc(w_in, 16)
            sp.dma_start(bvc[:, :], bv_cols).then_inc(w_in, 16)
            sp.dma_start(bor[:, :, :], bo_rows).then_inc(w_in, 16)
            load_x(1 * CHUNK, 1)
            load_ctx(0 * CHUNK, 2)
            load_ctx(1 * CHUNK, 3)
            load_masks(0 * CHUNK, 2)
            load_masks(1 * CHUNK, 3)
            sp.dma_start(cT[:, :], centro).then_inc(w1_in, 16)
            sp.dma_start(lng[:, :], ln_g).then_inc(w1_in, 16)
            sp.dma_start(lnb[:, :], ln_b).then_inc(w1_in, 16)
            sp.dma_start(w1raw[:, :, :], w1t.rearrange("e d f -> d e f")).then_inc(w1_in, 16)
            sp.dma_start(b1raw[:, :, :], b1c).then_inc(ffw_in, 16)
            for e in range(E):
                sp.dma_start(wpack[:, e, F:2 * F].rearrange("p (c d) -> p c d", c=FC),
                             w2t[e, :, :].rearrange("(c p) d -> p c d", p=P)).then_inc(ffw_in, 16)
                sp.dma_start(wpack[:, e, 2 * F + FC:WCOLS], b2[e:e + 1, :].to_broadcast([P, D])).then_inc(ffw_in, 16)

            with sp.Fori(0, ITERS - 1) as it:
                for k in range(2):
                    row = ((it + 1) * 2 + k) * CHUNK
                    sp.wait_ge(xn_ok, it * PH + (k + 3))
                    load_x(row, k)
                    sp.wait_ge(p_mm, written(it, k + 2, "C"))
                    load_ctx(row, k + 2)
                    sp.wait_ge(madd_ok, it * 2 + (k + 1))
                    load_masks(row, k + 2)

            sp.wait_ge(ffw_in, 16 * (1 + 2 * E))
            sp.wait_ge(scaled, 1)
            sp.wait_ge(scattered, 16 * NT)
            sp.wait_ge(et_ok, 1)
            sp.wait_ge(b1_ok, 1)

            def load_tile(tile, r):
                row = sp.snap(tile * P)
                expert = sp.value_load(et[0:1, bass.ds(tile, 1)], min_val=0, max_val=E - 1)
                col = sp.snap(expert * WCOLS)
                sp.dma_start(xt[r][:, :], xs_dram[bass.ds(row, P), :]).then_inc(xt_in[r], 16)
                sp.dma_start(wb[r][:, :], wflat[:, bass.ds(col, WCOLS)]).then_inc(wb_in[r], 16)

            def next_tiles(i, last):
                for j in range(FU):
                    sp.wait_ge(y_ok, i * FU + (j + 1 + Y0))
                    if not (last and j + RING >= FU):
                        load_tile(i * FU + (j + RING), j % RING)

            for j in range(RING):
                load_tile(j, j)
            with sp.Fori(0, FT // FU - 1) as i:
                next_tiles(i, False)
            next_tiles(FT // FU - 1, True)
            for r in range(RING):
                sp.wait_ge(yt_out[r], FT // RING * 16)
            for c in range(NT // 4):
                sp.dma_start(xhat[:, 4 * c:4 * c + 4, 0:D],
                             ys_dram[c * CHUNK:(c + 1) * CHUNK, :].rearrange("(u p) d -> p u d", p=P)).then_inc(yg_in[c], 16)
            for c in range(NT // 4):
                sp.wait_ge(out_ok, 4 * c + 4)
                sp.dma_start(out[c * CHUNK:(c + 1) * CHUNK, :].rearrange("(u p) d -> p u d", p=P),
                             x2[:, 4 * c:4 * c + 4, :]).then_inc(out_done, 16)
            sp.wait_ge(out_done, 16 * (NT // 4))

        @block.tensor
        def _(pe):
            def item(it, k, name):
                if name in "LA":
                    if k > PH - 1:
                        (transpose_rows if name == "L" else affinity)(it, k - 1)
                    else:
                        pe.wait_ge(p_read[pbank(k, name)], earlier_read(it, k, name))
                        pe.sem_inc(p_read[pbank(k, name)], 1)
                        pe.wait_ge(p_mm, written(it, k, name) - 1)
                        pe.sem_inc(p_mm, 1)
                    return
                par, bk = k % 2, bankP[pbank(k, name)]
                if place(k, name) > 1 or k > 0:
                    pe.wait_ge(p_read[pbank(k, name)], earlier_read(it, k, name))
                self_attn = k % PH < 2
                src = xnT if self_attn else cxT
                if name == "T":
                    pe.wait_ge(xn_ok, it * PH + (k + 1))
                    for u in range(UNITS):
                        last = nc.tensor.transpose(bk[:, u * P:(u + 1) * P], xn[:, u, :], ident)
                elif name == "C":
                    pe.wait_ge(c_in[par], it * 16 + 16)
                    for u in range(UNITS):
                        last = nc.tensor.transpose(bk[:, u * P:(u + 1) * P], cin[par][:, u, :], ident)
                elif name[0] == "S":
                    part, g = "KQ".index(name[1]), int(name[2])
                    if g == 0:
                        pe.wait_ge(hi_ok, it * (PH * 2) + (k * 2 + part + 1))
                        pe.wait_ge(lo_ok, it * (PH * 2) + (k * 2 + part + 1))
                    for hl, halves in enumerate((phi[part], plo[part])):
                        last = nc.tensor.matmul(bk[0:STK, :], sel16[:, part, hl, g, :], halves[:, :], start=hl == 0, stop=hl == 1)
                elif name in ("V0", "V1"):
                    for j in range(4):
                        seq = 4 * int(name[1]) + j
                        last = nc.tensor.matmul(bk[:, j * D:(j + 1) * D], src[:, seq, :, :].rearrange("p a s -> p (a s)"),
                                                w[:, WV if self_attn else XV, :], start=True, stop=True)
                else:
                    for n in {"K": ("T",) if self_attn else ("C",), "Q": () if self_attn else ("T",)}.get(name, ()):
                        pe.wait_ge(p_read[pbank(k, n)], read_out(it, k, n))
                    wi = {"Q": WQ, "Qr": WQR, "K": WK, "Kr": WKR}[name] if self_attn else {"Q": XQ, "K": XK}[name]
                    last = nc.tensor.matmul(bk[:, :].rearrange("p (b s) -> p b s", b=SEQS), w[:, wi, :], (xnT if name[0] == "Q" else src)[:, :, 0, :], start=True, stop=True)
                last.then_inc(p_mm, 1)

            UB = PH * UNITS

            def bank_for(it, k, name):
                kk, nm = finish_place(it, k, name)
                pe.wait_ge(p_read[pbank(kk, nm)], earlier_read(it, kk, nm))
                return bankP[pbank(kk, nm)]

            def transpose_rows(it, k):
                bk = bank_for(it, k, "L")
                pe.wait_ge(xl_ok, finished(it, k))
                for u in range(UNITS):
                    last = nc.tensor.transpose(bk[:, u * P:(u + 1) * P], xl[:, u, :], ident)
                last.then_inc(p_mm, 1)

            def affinity(it, k):
                bk = bank_for(it, k, "A")
                kl, nl = finish_place(it, k, "L")
                pe.wait_ge(p_read[pbank(kl, nl)], read_out(it, kl, nl))
                for u in range(UNITS):
                    last = nc.tensor.matmul(bk[:, u * E:(u + 1) * E], xlT[:, u, :], cT[:, :], start=True, stop=True)
                last.then_inc(p_mm, 1)

            def scores(it, k, u):
                par = k % 2
                if u == 0 and k % PH > 1:
                    pe.wait_ge(madd_ok, it * 2 + (k - 1))
                if u < 2:
                    pe.wait_ge(kbd_ok, it * (PH * 2) + (2 * k + u + 1))
                if u == 0:
                    for name in ("SQ2", "SQ3"):
                        pe.wait_ge(p_read[pbank(k, name)], read_out(it, k, name))
                for h in range(2):
                    if k > 0 or u > 0:
                        pe.wait_ge(mx_ok, it * 2 * UB + (2 * (k * UNITS + u) - 1 + h))
                    cross = k % PH > 1
                    if cross:
                        nc.tensor.matmul(bankA[h][:, :], idb[:, :], madd[par][:, 0, u, :].unsqueeze(1).broadcast_to([P, 8, S]),
                                         start=True, stop=False, skip_group_check=True)
                    for gl in range(2):
                        g = 2 * h + gl
                        for b in range(2):
                            tok = slice(u * P + b * S, u * P + (b + 1) * S)
                            last = nc.tensor.matmul(
                                bankA[h][b * S:(b + 1) * S, gl * 256:(gl + 1) * 256], qs[par][:, g, tok],
                                kbd[par][:, g, 2 * u + b, :, :].rearrange("p s t -> p (s t)"), start=not cross, stop=True, skip_group_check=cross)
                    last.then_inc(a_mm, 1)

            def scores_t(it, k, u, b):
                par = k % 2
                if b == 0:
                    pe.wait_ge(mx_ok, it * 2 * UB + 2 * (k * UNITS + u + 1))
                pe.wait_ge(exp_ok, it * 2 * UB + (2 * (k * UNITS + u) + b - 1 + EXP0))
                tok = slice(u * P + b * S, u * P + (b + 1) * S)
                for pr in range(PAIRS):
                    for t in range(2):
                        nc.tensor.matmul(bankB[b][t * S:(t + 1) * S, pr * S:(pr + 1) * S],
                                         mx[u % 2][:, 2 * pr + t:2 * pr + t + 1].broadcast_to([P, S]),
                                         negid[:, b * S:(b + 1) * S], start=(pr == 0), stop=False, skip_group_check=True)
                for pr in range(PAIRS):
                    g, s0 = pr // 2, 2 * (pr % 2)
                    last = nc.tensor.matmul(bankB[b][:, pr * S:(pr + 1) * S], kbd[par][:, g, 2 * u + b, s0:s0 + 2, :].rearrange("p s t -> p (s t)"),
                                            qs[par][:, g, tok], start=False, stop=(pr == PAIRS - 1), skip_group_check=True)
                if k % PH > 1:
                    last = nc.tensor.matmul(bankB[b][:, :], dupid[b][:, :, :].rearrange("p a s -> p (a s)"),
                                            madd[par][:, 1, u, :].unsqueeze(1).broadcast_to([P, PAIRS, S]),
                                            start=False, stop=True, skip_group_check=True)
                last.then_inc(b_mm, 1)

            def attend(it, k, u):
                par = k % 2
                if u % 2 == 0:
                    name = "V1" if u else "V0"
                    pe.wait_ge(p_read[pbank(k, name)], read_out(it, k, name))
                pe.wait_ge(on_ok, it * UB + (k * UNITS + u + START))
                for b in range(2):
                    pe.wait_ge(exp_ok, it * 2 * UB + (2 * (k * UNITS + u) + b + 1 + EXP0))
                    for pr in range(PAIRS):
                        last = nc.tensor.matmul(bankO[b * S:(b + 1) * S, pr * 18:(pr + 1) * 18],
                                                prob[(2 * u + b) % 4][:, pr * S:(pr + 1) * S],
                                                v9[par][:, 2 * u + b, pr, :, :].rearrange("p a d -> p (a d)"), start=True, stop=True)
                    last.then_inc(pv_mm, 1)

            def out_transpose(it, k, u):
                pe.wait_ge(on_ok, it * UB + (k * UNITS + u + 1 + START))
                pe.wait_ge(res_ok, it * UB + (k * UNITS + u + START))
                nc.tensor.transpose(bankY[:, 0:P], on[:, :, :].rearrange("p h d -> p (h d)"), ident).then_inc(ot_mm, 1)

            def out_project(it, k, u):
                pe.wait_ge(ot_ok, it * UB + (k * UNITS + u + 1))
                nc.tensor.matmul(bankY[:, P:2 * P], onT[:, :], w[:, WO if k % PH < 2 else XO, :],
                                 start=True, stop=True).then_inc(wo_mm, 1)

            def hidden_bias(e0, e1):
                pe.wait_ge(w1_in, 64)
                for e in range(e0, e1):
                    for c in range(FC):
                        last = nc.tensor.matmul(bankO[:, B1_COL + e * FC + c:B1_COL + e * FC + c + 1],
                                                w1raw[:, e, c * P:(c + 1) * P], lnb[:, e:e + 1], start=True, stop=True)
                last.then_inc(b1_mm, 1)

            pe.sem_inc(pv_mm, PV0)
            for s in (ot_mm, b_mm, h_mm):
                pe.sem_inc(s, START)
            pe.sem_inc(y_mm, Y0)
            pe.wait_ge(w_in, 80)
            pe.wait_ge(setup_dve, 8)
            for a in range(2):
                nc.tensor.matmul(bankY[:, a * P:(a + 1) * P], bvc[:, a:a + 1].broadcast_to([P, P]), w[:, WO if a == 0 else XO, :],
                                 start=True, stop=False)
                last = nc.tensor.matmul(bankY[:, a * P:(a + 1) * P], ones[0:1, :], bor[0:1, a, :], start=False, stop=True)
            last.then_inc(bo_mm, 1)
            for name in items(0)[:-1]:
                item(0, 0, name)
            scores(0, 0, 0)
            pe.wait_ge(bo_done, 1)

            hidden_bias(0, E // 2)

            def phase(it, k, last=False):
                for u in range(UNITS):
                    ahead = not last
                    scores_t(it, k, u, 0)
                    if k or u:
                        out_transpose(it, *((k, u - 1) if u else (k - 1, UNITS - 1)))
                    scores_t(it, k, u, 1)
                    if k or u:
                        out_project(it, *((k, u - 1) if u else (k - 1, UNITS - 1)))
                    if last and u == 3:
                        transpose_rows(it, k)
                    for name in step_items(k + 1, u, 0) if ahead else ():
                        item(it, k + 1, name)
                    if ahead or u < UNITS - 1:
                        scores(it, k + (u + 1) // UNITS, (u + 1) % UNITS)
                    for name in step_items(k + 1, u, 1) if ahead else ():
                        item(it, k + 1, name)
                    attend(it, k, u)
                    if last and u == 3:
                        affinity(it, k)
                    if u == 0:
                        item(it, k, "V1")
                    for name in step_items(k + 1, u, 2) if ahead else ():
                        item(it, k + 1, name)

            phase(0, 0)
            with pe.Fori(0, ITERS - 1) as it:
                for k in range(1, PH + 1):
                    phase(it, k)
            for k in range(1, PH):
                phase(ITERS - 1, k, k == PH - 1)
            out_transpose(ITERS - 1, PH - 1, UNITS - 1)
            out_project(ITERS - 1, PH - 1, UNITS - 1)
            transpose_rows(ITERS - 1, PH)
            affinity(ITERS - 1, PH)

            pe.wait_ge(oh_ok, 1)
            nc.tensor.matmul(bankP[0][:, 0:E * NT], tri, oh[:, :, :].rearrange("p e t -> p (e t)"), start=True, stop=True)
            nc.tensor.matmul(bankP[1][:, 0:E * NT], ones[:, :], oh[:, :, :].rearrange("p e t -> p (e t)"),
                             start=True, stop=True).then_inc(rank_mm, 1)

            pe.wait_ge(on_ok, NT * 2 + START)
            hidden_bias(E // 2, E)

            pe.wait_ge(b1_ok, 1)

            def up_t(i, j):
                pe.wait_ge(xt_in[j % RING], i * (FU // RING * 16) + (j // RING + 1) * 16)
                pe.wait_ge(xtT_ok, i * FU + (j - 1 + XT0))
                nc.tensor.transpose(bankA[j % 2][:, 0:P], xt[j % RING][:, 0:D], ident).then_inc(xtT_mm, 1)

            def up(i, j):
                pe.wait_ge(xtT_ok, i * FU + (j + 1 + XT0))
                pe.wait_ge(wb_in[j % RING], i * (FU // RING * 16) + (j // RING + 1) * 16)
                pe.wait_ge(relu_act, i * FU + (j - 1 + RELU0))
                pe.wait_ge(relu_dve, i * FU + (j - 1 + Y0))
                for c in range(FC):
                    dst = (bankB, bankP)[c // 2][j % 2]
                    last = nc.tensor.matmul(dst[:, (c % 2) * P:(c % 2 + 1) * P], wb[j % RING][:, c * P:(c + 1) * P], xtT[j % 2][:, :],
                                            start=True, stop=True)
                last.then_inc(h_mm, 1)

            def down(i, j):
                pe.wait_ge(relu_act, i * FU + (j + 1 + RELU0))
                pe.wait_ge(relu_dve, i * FU + (j + 1 + Y0))
                pe.wait_ge(y_ok, i * FU + (j - 1 + Y0))
                dst = (bankO, bankY)[j % 2]
                for c in range(FC):
                    last = nc.tensor.matmul(dst[:, 0:D], hT[j % 2][:, c, :], wb[j % RING][:, F + c * P:F + (c + 1) * P],
                                            start=(c == 0), stop=(c == FC - 1))
                last.then_inc(y_mm, 1)

            def tiles(i, last):
                for j in range(FU):
                    if not (last and j + 2 >= FU):
                        up_t(i, j + 2)
                    if not (last and j + 1 >= FU):
                        up(i, j + 1)
                    down(i, j)

            up_t(0, 0)
            up_t(0, 1)
            up(0, 0)
            with pe.Fori(0, FT // FU - 1) as i:
                tiles(i, False)
            tiles(FT // FU - 1, True)

        @block.scalar
        def _(act):
            UB = PH * UNITS
            act.sem_inc(xhat_ok, START)
            act.sem_inc(exp_ok, EXP0)
            act.sem_inc(xtT_ok, XT0)
            act.sem_inc(relu_act, RELU0)
            act.wait_ge(w_in, 80)

            def copy_rows(it, k, name, dst):
                act.wait_ge(p_mm, written(it, k, name))
                nc.scalar.activation(dst[:, :, :, :], bankP[pbank(k, name)][:, :].rearrange("p (b s) -> p b s", b=SEQS)
                                     .unsqueeze(2).broadcast_to([P, SEQS, 2, S]), ACT.Copy).then_inc(p_read[pbank(k, name)], 1)

            def high(it, k, part):
                name = "KQ"[part]
                if k % PH < 2:
                    act.wait_ge(rope_ok, it * 4 + (2 * (k if k < 2 else k - 2) + part + 1))
                    nc.scalar.activation(phi[part][:, :], p32[part][:, :], ACT.Copy).then_inc(hi_ok, 1)
                else:
                    bk = bankP[pbank(k, name)]
                    bias = bcol[:, 5 - part:6 - part]
                    act.wait_ge(p_mm, written(it, k, name))
                    nc.scalar.activation(phi[part][:, :], bk[:, :], ACT.Identity, bias=bias).then_inc(hi_ok, 1)
                    act.wait_ge(lo_ok, it * (PH * 2) + (k * 2 - 1 + part))
                    nc.scalar.activation(p32[part][:, :], bk[:, :], ACT.Identity, bias=bias).then_inc(p_read[pbank(k, name)], 1)

            def values(it, k, name):
                bk, j = bankP[pbank(k, name)], int(name[1])
                if k > 0:
                    act.wait_ge(pv_mm, it * 2 * UB + ((k - 1) * 2 * UNITS + PV0))
                act.wait_ge(p_mm, written(it, k, name))
                src = bk[:, :].rearrange("p (b r t d) -> p b r t d", b=4, r=PAIRS, t=2)
                for t in range(2):
                    half = slice(t * S, (t + 1) * S)
                    ins = nc.scalar.activation(v9[k % 2][half, 4 * j:4 * j + 4, :, t, 0:HD], src[half, :, :, t, :], ACT.Copy)
                ins.then_inc(p_read[pbank(k, name)], 1)

            def stack(it, k, name):
                bk, g = bankP[pbank(k, name)], int(name[2])
                act.wait_ge(p_mm, written(it, k, name))
                nc.scalar.activation((ks if name[1] == "K" else qs[k % 2])[:, g, :], bk[0:STK, :], ACT.Copy)\
                    .then_inc(p_read[pbank(k, name)], 1)

            def copy_rows_t(it, k):
                kk, nm = finish_place(it, k, "L")
                act.wait_ge(p_mm, written(it, kk, nm))
                nc.scalar.activation(xlT[:, :, :].rearrange("p a d -> p (a d)"), bankP[pbank(kk, nm)][:, :], ACT.Copy)\
                    .then_inc(p_read[pbank(kk, nm)], 1)

            def exps(it, k, u, b):
                act.wait_ge(b_mm, it * 2 * UB + (2 * (k * UNITS + u) + b + 1 + START))
                act.wait_ge(pv_mm, it * 2 * UB + (2 * (k * UNITS + u) + b - 3 + PV0))
                nc.scalar.activation(prob[(2 * u + b) % 4][:, :], bankB[b][:, :], ACT.Exp, scale=SCALE).then_inc(exp_ok, 1)

            def prepare(it, k, names):
                for name in names:
                    if name == "T":
                        copy_rows(it, k, name, xnT)
                    elif name == "C":
                        copy_rows(it, k, name, cxT)
                    elif name in ("K", "Q"):
                        high(it, k, 0 if name == "K" else 1)
                    elif name in ("SK0", "SK1", "SK2", "SK3", "SQ0", "SQ1", "SQ2", "SQ3"):
                        stack(it, k, name)
                    elif name == "L" and k > PH - 1:
                        copy_rows_t(it, k - 1)
                    elif name in ("V0", "V1"):
                        values(it, k, name)

            act.wait_ge(bo_mm, 1)
            nc.scalar.activation(bo_eff[:, :, :].rearrange("p a d -> p (a d)"), bankY[:, 0:2 * P], ACT.Copy).then_inc(bo_done, 1)
            act.wait_ge(v9_ok, 1)
            prepare(0, 0, items(0)[:-1])

            def expert_rows(it, k):
                for u in range(UNITS):
                    ins = nc.scalar.activation(
                        xhat[:, bass.ds(it * (2 * UNITS) + ((k - 3) * UNITS + u), 1), 0:D].rearrange("p a d -> p (a d)"),
                        xl[:, u, :], ACT.Copy, scale=r2[:, u:u + 1])
                ins.then_inc(xhat_ok, 1)

            def phase(it, k, last=False):
                for u in range(UNITS):
                    ahead = not last
                    exps(it, k, u, 0)
                    if ahead and u == 2:
                        prepare(it, k + 1, ["K"])
                    exps(it, k, u, 1)
                    if u == 0:
                        values(it, k, "V1")
                    if last and u == 3:
                        copy_rows_t(it, k)
                    if ahead:
                        prepare(it, k + 1, step_items(k + 1, u, 0) + step_items(k + 1, u, 1))
                    if k > 2 and u == 3:
                        expert_rows(it, k)
                    if ahead:
                        prepare(it, k + 1, [n for n in step_items(k + 1, u, 2) if n != "K"])

            phase(0, 0)
            with act.Fori(0, ITERS - 1) as it:
                for k in range(1, PH + 1):
                    phase(it, k)
            for k in range(1, PH):
                phase(ITERS - 1, k, k == PH - 1)
            copy_rows_t(ITERS - 1, PH)
            expert_rows(ITERS - 1, PH)
            act.wait_ge(amax_ok, 1)
            nc.scalar.activation(alpha[:, :], amax[:, :], ACT.Exp, scale=-1.0).then_inc(sig_ok, 1)

            def copy_tile_t(i, j):
                act.wait_ge(xtT_mm, i * FU + (j + 1))
                if j > 0:
                    act.wait_ge(h_mm, i * FU + (j - 1 + START))
                nc.scalar.activation(xtT[j % 2][:, :], bankA[j % 2][:, 0:P], ACT.Copy).then_inc(xtT_ok, 1)

            def hidden_act(i, j):
                act.wait_ge(h_mm, i * FU + (j + 1 + START))
                act.wait_ge(y_mm, i * FU + (j - 1 + Y0))
                for c in range(2):
                    ins = nc.scalar.activation(hT[j % 2][:, c, :], bankB[j % 2][:, c * P:(c + 1) * P], ACT.Relu,
                                               bias=wb[j % RING][:, 2 * F + c:2 * F + c + 1])
                ins.then_inc(relu_act, 1)

            def tiles(i, last):
                for j in range(FU):
                    if not (last and j + 1 >= FU):
                        copy_tile_t(i, j + 1)
                    hidden_act(i, j)

            copy_tile_t(0, 0)
            with act.Fori(0, FT // FU - 1) as i:
                tiles(i, False)
            tiles(FT // FU - 1, True)

        @block.vector
        def _(dve):
            UB = PH * UNITS
            for s in (on_ok, res_ok):
                dve.sem_inc(s, START)
            for i in range(2):
                nc.vector.memset(v9[i][:, :, :, :, :], 0.0).then_inc(v9_zero, 1)
            dve.wait_ge(v9_zero, 2)
            for i in range(2):
                for t in range(2):
                    ins = nc.vector.memset(v9[i][t * S:(t + 1) * S, :, :, t, HD], 1.0)
            ins.then_inc(v9_ok, 1)
            nc.vector.memset(sel16[:, :, :, :, :], 0.0).then_inc(sel_zero, 1)
            nc.vector.memset(ones[:, :], 1.0).then_inc(setup_dve, 1)
            dve.wait_ge(w_in, 80)
            nc.vector.tensor_scalar(negid[:, :], ident, -1.0, None, ALU.mult).then_inc(setup_dve, 1)
            nc.vector.tensor_copy(idb[:, :], ident).then_inc(setup_dve, 1)
            for b in range(2):
                for t in range(2):
                    nc.vector.tensor_copy(dupid[b][:, t, :], cst[:, C_ID + b * S:C_ID + (b + 1) * S]).then_inc(setup_dve, 1)

            dve.wait_ge(sel_zero, 1)
            for part, blocks in enumerate((((0, 2), (1,)), ((0, 1), (2,)))):
                for hl in range(2):
                    for blk in blocks[hl]:
                        ins = nc.vector.tensor_copy(sel16[:, part, hl, :, 32 * blk:32 * blk + 32],
                                                    ident.rearrange("p (g r) -> p g r", g=GROUPS))
            ins.then_inc(setup_dve, 1)

            def rows(k, u):
                return (xin if k % PH < 2 else x1)[k % 2][:, u, :]

            def row_stats(it, k, u):
                if k % PH < 2:
                    if u == 0:
                        dve.wait_ge(x_in[k % 2], it * 16 + (k // PH + 1) * 16)
                else:
                    dve.wait_ge(res_ok, it * UB + ((k - 2) * UNITS + u + 1 + START))
                ins = nc.vector.bn_stats(stats[:, u, :], rows(k, u))
                if u == UNITS - 1:
                    ins.then_inc(ln_own, 1)

            def moments(it, k):
                dve.wait_ge(ln_own, it * PH + (k + 1))
                nc.vector.memset(scratch[:, 0:1], 0.0).then_inc(spare, 1)
                for u in range(UNITS):
                    ins = nc.vector.bn_aggr(mv[:, u, :], stats[:, u, :])
                ins.then_inc(ln_stats, 1)

            def norm(it, k):
                if k > 0:
                    dve.wait_ge(p_mm, written(it, k - 1, "T"))
                dve.wait_ge(rstd_ok, it * PH + (k + 1))
                for u in range(UNITS):
                    ins = nc.vector.tensor_scalar(xn[:, u, :], rows(k, u), mv[:, u, 0:1], rstd[:, u:u + 1], ALU.subtract, ALU.mult)
                ins.then_inc(xn_ok, 1)

            def rotate(it, k, name):
                part = 0 if name[0] == "K" else 1
                if name in ("K", "Q") and k > 0:
                    dve.wait_ge(lo_ok, it * (PH * 2) + (2 * k - 1 + part))
                dve.wait_ge(p_mm, written(it, k, name))
                rot = len(name) > 1
                bi = {"Q": 0, "Qr": 1, "K": 2, "Kr": 3}[name]
                col = C_SIN if rot else C_COS
                nc.vector.scalar_tensor_tensor(
                    (t_sin if rot else p32)[part][:, :].rearrange("p (b s) -> p b s", b=SEQS),
                    bankP[pbank(k, name)][:, :].rearrange("p (b s) -> p b s", b=SEQS), bcol[:, bi:bi + 1],
                    cst[:, col:col + S].unsqueeze(1).broadcast_to([P, SEQS, S]), ALU.add, ALU.mult).then_inc(p_read[pbank(k, name)], 1)

            def mask_terms(it, k):
                dve.wait_ge(m_in[k % 2], it * 32 + 32)
                dve.wait_ge(b_mm, it * 2 * UB + ((k - 1) * 2 * UNITS + START))
                nc.vector.tensor_scalar(madd[k % 2][:, :, :, :], mraw[k % 2][:, :, :, :], 0.0, MASKED, ALU.is_equal, ALU.mult)\
                    .then_inc(madd_ok, 1)

            def mask_keys(it, k, rest):
                if not rest:
                    for name in ("SK2", "SK3"):
                        dve.wait_ge(p_read[pbank(k, name)], read_out(it, k, name))
                    if k > 0:
                        dve.wait_ge(b_mm, it * 2 * UB + ((k - 1) * 2 * UNITS + START))
                seqs = slice(2, SEQS) if rest else slice(0, 2)
                for s in range(GH):
                    ins = nc.vector.tensor_scalar(kbd[k % 2][:, :, seqs, s, :],
                                                  ks[:, :, :].rearrange("p g (b t) -> p g b t", b=SEQS)[:, :, seqs, :],
                                                  cst[0:STK, C_MASK + s:C_MASK + s + 1], None, ALU.mult)
                ins.then_inc(kbd_ok, 1)

            def maxima(it, k, u):
                if k > 0 or u > 0:
                    dve.wait_ge(b_mm, it * 2 * UB + (2 * (k * UNITS + u) - 2 + START))
                for h in range(2):
                    dve.wait_ge(a_mm, it * 2 * UB + (2 * (k * UNITS + u) + h + 1))
                    nc.vector.tensor_reduce(mx[u % 2][:, 8 * h:8 * h + 8], bankA[h][:, :].rearrange("p (h t) -> p h t", t=S),
                                            AX.X, ALU.max).then_inc(mx_ok, 1)

            def normalise(it, k, u):
                dve.wait_ge(pv_mm, it * 2 * UB + (2 * (k * UNITS + u) + 2 + PV0))
                o9 = bankO[:, 0:H * 9].rearrange("p (h d) -> p h d", h=H)
                nc.vector.reciprocal(rden[:, :], o9[:, :, HD]).then_inc(rden_ok, 1)
                dve.wait_ge(rden_ok, it * UB + (k * UNITS + u + 1))
                dve.wait_ge(ot_mm, it * UB + (k * UNITS + u + START))
                nc.vector.tensor_tensor(on[:, :, :], o9[:, :, 0:HD], rden[:, :].unsqueeze(2).broadcast_to([P, H, HD]),
                                        ALU.mult).then_inc(on_ok, 1)

            def stack(it, k, name):
                bk, g = bankP[pbank(k, name)], int(name[2])
                dve.wait_ge(p_mm, written(it, k, name))
                nc.vector.tensor_copy((ks if name[1] == "K" else qs[k % 2])[:, g, :], bk[0:STK, :])\
                    .then_inc(p_read[pbank(k, name)], 1)

            def copy_out_t(it, k, u):
                dve.wait_ge(ot_mm, it * UB + (k * UNITS + u + 1 + START))
                nc.vector.tensor_copy(onT[:, :], bankY[:, 0:P]).then_inc(ot_ok, 1)

            def residual(it, k, u):
                dve.wait_ge(wo_mm, it * UB + (k * UNITS + u + 1))
                if u == 0:
                    dve.wait_ge(xb_ok, it * PH + (k + 1))
                if k % PH < 2:
                    dst = x1[k % 2][:, u, :]
                else:
                    dst = x2[:, bass.ds(it * (2 * UNITS) + ((k % 2) * UNITS + u), 1), :].rearrange("p a d -> p (a d)")
                nc.vector.tensor_tensor(dst, bankY[:, P:2 * P], xb[k % 2][:, u, :], ALU.add).then_inc(res_ok, 1)

            for u in range(UNITS):
                row_stats(0, 0, u)
            moments(0, 0)
            norm(0, 0)
            for name in ("K", "Kr", "Q", "Qr"):
                rotate(0, 0, name)
            mask_keys(0, 0, False)
            mask_keys(0, 0, True)
            maxima(0, 0, 0)

            def out_stats(it, k, u):
                dve.wait_ge(res_ok, it * UB + (k * UNITS + u + 1 + START))
                nc.vector.memset(scratch[:, 1:2], 0.0).then_inc(spare, 1)
                ins = nc.vector.bn_stats(stat3[:, u, :], x2[:, bass.ds(it * (2 * UNITS) + ((k % 2) * UNITS + u), 1), :]
                                         .rearrange("p a d -> p (a d)"))
                if u == UNITS - 1:
                    ins.then_inc(mv3_own, 1)

            def out_moments(it, k):
                dve.wait_ge(mv3_own, finished(it, k))
                nc.vector.memset(scratch[:, 2:3], 0.0).then_inc(spare, 1)
                for u in range(UNITS):
                    ins = nc.vector.bn_aggr(mv3[:, u, :], stat3[:, u, :])
                ins.then_inc(mv3_ok, 1)

            def third_norm(it, k):
                dve.wait_ge(b1_mm, 1)
                dve.wait_ge(scaled, 1)
                dve.wait_ge(xhat_ok, finished(it, k) - 1 + START)
                dve.wait_ge(base_ok, finished(it, k) - 1 + START)
                dve.wait_ge(r_ok, finished(it, k))
                for u in range(UNITS):
                    ins = nc.vector.tensor_scalar(xl[:, u, :], x2[:, bass.ds(it * (2 * UNITS) + ((k - 3) * UNITS + u), 1), :]
                                                  .rearrange("p a d -> p (a d)"), mv3[:, u, 0:1], r1[:, u:u + 1],
                                                  ALU.subtract, ALU.mult)
                ins.then_inc(xl_ok, 1)

            def copy_affinity(it, k):
                kk, nm = finish_place(it, k, "A")
                dve.wait_ge(p_mm, written(it, kk, nm))
                nc.vector.tensor_copy(aff[:, bass.ds(it * (2 * UNITS) + (k - 3) * UNITS, UNITS), :],
                                      bankP[pbank(kk, nm)][:, 0:UNITS * E].rearrange("p (u e) -> p u e", e=E))\
                    .then_inc(p_read[pbank(kk, nm)], 1)

            def stats_unit(it, pk, pu):
                if pk % PH < 2:
                    row_stats(it, pk + 2, pu)
                else:
                    out_stats(it, pk, pu)

            def phase(it, k, last=False, more=True):
                for u in range(UNITS):
                    ahead = not last
                    pk, pu = (k, u - 1) if u else (k - 1, UNITS - 1)
                    if k or u:
                        copy_out_t(it, pk, pu)
                        residual(it, pk, pu)
                    if ahead and u == 2 and (k + 1) % PH < 2:
                        rotate(it, k + 1, "Q")
                        rotate(it, k + 1, "Qr")
                    if ahead and u == UNITS - 1:
                        mask_keys(it, k + 1, False)
                    if ahead or u < UNITS - 1:
                        maxima(it, k + (u + 1) // UNITS, (u + 1) % UNITS)
                    if k or u:
                        stats_unit(it, pk, pu)
                    if ahead and u == 0:
                        moments(it, k + 1)
                    normalise(it, k, u)
                    if k > 2 and u == 0:
                        out_moments(it, k)
                    if k > 2 and u == 2:
                        third_norm(it, k)
                    if k > 2 and u == 3:
                        copy_affinity(it, k)
                    if ahead:
                        if u == 0:
                            norm(it, k + 1)
                        if u == 1 and (k + 1) % PH < 2:
                            rotate(it, k + 1, "K")
                            rotate(it, k + 1, "Kr")
                        if u == 1 and (k + 1) % PH > 1:
                            mask_terms(it, k + 1)
                        if u == 2 and (k + 2) % PH < 2 and more:
                            for v in range(UNITS):
                                row_stats(it, k + 2, v)
                        if u == UNITS - 1:
                            mask_keys(it, k + 1, True)

            for u in range(UNITS):
                row_stats(0, 1, u)
            phase(0, 0)
            with dve.Fori(0, ITERS - 1) as it:
                for k in range(1, PH + 1):
                    phase(it, k)
            for k in range(1, PH):
                phase(ITERS - 1, k, k == PH - 1, False)
            copy_out_t(ITERS - 1, PH - 1, UNITS - 1)
            residual(ITERS - 1, PH - 1, UNITS - 1)
            stats_unit(ITERS - 1, PH - 1, UNITS - 1)
            out_moments(ITERS - 1, PH)
            third_norm(ITERS - 1, PH)
            copy_affinity(ITERS - 1, PH)

            step = [0]

            def chained(ins):
                step[0] += 1
                ins.then_inc(route, 1)
                dve.wait_ge(route, step[0])

            kk, nm = finish_place(ITERS - 1, PH, "A")
            dve.wait_ge(p_read[pbank(kk, nm)], read_out(ITERS - 1, kk, nm))
            nc.vector.tensor_reduce(amax[:, :], aff[:, :, :], AX.X, ALU.max).then_inc(amax_ok, 1)
            dve.wait_ge(amax_ok, 1)
            chained(nc.vector.tensor_tensor(eq[:, :, :], aff[:, :, :], amax[:, :].unsqueeze(2).broadcast_to([P, NT, E]), ALU.is_ge))
            chained(nc.vector.tensor_tensor(eq[:, :, :], eq[:, :, :], cst[:, C_RANK:C_RANK + E].unsqueeze(1).broadcast_to([P, NT, E]),
                                            ALU.mult))
            chained(nc.vector.tensor_reduce(sel[:, :], eq[:, :, :], AX.X, ALU.max))
            nc.vector.tensor_tensor(oh[:, :, :], sel[:, :].unsqueeze(1).broadcast_to([P, E, NT]),
                                    cst[:, C_RANK:C_RANK + E].unsqueeze(2).broadcast_to([P, E, NT]), ALU.is_equal).then_inc(oh_ok, 1)
            dve.wait_ge(rank_mm, 1)
            nc.vector.tensor_copy(pre[:, :, :].rearrange("p e t -> p (e t)"), bankP[0][:, 0:E * NT])
            chained(nc.vector.tensor_copy(tot[:, :, :].rearrange("p e t -> p (e t)"), bankP[1][:, 0:E * NT]))
            chained(nc.vector.tensor_tensor_scan(inc[:, :, :].rearrange("p e t -> p (e t)"), cst[:, C_SEG:C_SEG + E * NT],
                                                 tot[:, :, :].rearrange("p e t -> p (e t)"), 0.0, ALU.mult, ALU.add))
            chained(nc.vector.tensor_scalar(gt[:, :], cst[:, C_IOTA:C_IOTA + NT], float(P), None, ALU.mult))
            chained(nc.vector.tensor_tensor(gt2[:, :, :], inc[:, :, NT - 1].unsqueeze(2).broadcast_to([P, E, NT]),
                                            gt[:, :].unsqueeze(1).broadcast_to([P, E, NT]), ALU.is_gt))
            chained(nc.vector.tensor_reduce(ntile[:, :], gt2[:, :, :], AX.X, ALU.add))
            chained(nc.vector.tensor_tensor_scan(tinc[:, :], ones[:, 0:E], ntile[:, :], 0.0, ALU.mult, ALU.add))
            chained(nc.vector.tensor_tensor(texc[:, :], tinc[:, :], ntile[:, :], ALU.subtract))
            chained(nc.vector.tensor_tensor(inc[:, :, :], inc[:, :, :], tot[:, :, :], ALU.subtract))
            chained(nc.vector.tensor_tensor(inc[:, :, :], inc[:, :, :], pre[:, :, :], ALU.add))
            chained(nc.vector.scalar_tensor_tensor(inc[:, :, :], texc[:, :].unsqueeze(2).broadcast_to([P, E, NT]), float(P),
                                                   inc[:, :, :], ALU.mult, ALU.add))
            chained(nc.vector.tensor_tensor(inc[:, :, :], inc[:, :, :], oh[:, :, :], ALU.mult))
            chained(nc.vector.tensor_reduce(posf[:, :], inc[:, :, :].rearrange("p e t -> p t e"), AX.X, ALU.add))
            nc.vector.tensor_copy(pos[:, :], posf[:, :]).then_inc(rank_ok, 1)
            chained(nc.vector.tensor_tensor(geq[:, :, :], cst[:, C_IOTA:C_IOTA + FT].unsqueeze(2).broadcast_to([P, FT, E]),
                                            tinc[:, :].unsqueeze(1).broadcast_to([P, FT, E]), ALU.is_ge))
            chained(nc.vector.tensor_reduce(etf[:, :], geq[:, :, :], AX.X, ALU.add))
            chained(nc.vector.tensor_scalar(etf[:, :], etf[:, :], float(E - 1), None, ALU.min))
            nc.vector.tensor_copy(et[:, :], etf[:, :]).then_inc(et_ok, 1)
            dve.wait_ge(b1_mm, 2)
            nc.vector.tensor_tensor(wpack[:, :, 2 * F:2 * F + FC], bankO[:, B1_COL:B1_COL + E * FC].rearrange("p (e c) -> p e c", e=E),
                                    b1raw[:, :, :], ALU.add).then_inc(b1_ok, 1)
            dve.wait_ge(sig_ok, 1)
            chained(nc.vector.tensor_scalar(amax[:, :], alpha[:, :], 1.0, None, ALU.add))
            chained(nc.vector.reciprocal(alpha[:, :], amax[:, :]))

            dve.sem_inc(relu_dve, Y0)
            dve.sem_inc(y_ok, Y0)

            def hidden(i, j):
                dve.wait_ge(h_mm, i * FU + (j + 1 + START))
                dve.wait_ge(y_mm, i * FU + (j - 1 + Y0))
                for c in range(2, FC):
                    ins = nc.vector.tensor_scalar(hT[j % 2][:, c, :], bankP[j % 2][:, (c - 2) * P:(c - 1) * P],
                                                  wb[j % RING][:, 2 * F + c:2 * F + c + 1], 0.0, ALU.add, ALU.max)
                ins.then_inc(relu_dve, 1)

            def result(i, j, reused=True):
                dve.wait_ge(y_mm, i * FU + (j + 1 + Y0))
                if reused:
                    dve.wait_ge(yt_taken, i * FU + (j - (RING - 1)))
                    dve.wait_ge(yt_out[j % RING], i * (FU // RING * 16) + j // RING * 16)
                nc.vector.tensor_tensor(yt[j % RING][:, 0:D], (bankO, bankY)[j % 2][:, 0:D], wb[j % RING][:, 2 * F + FC:WCOLS], ALU.add)
                nc.vector.tensor_copy(yt[j % RING][:, D:D + 1].bitcast(i32), xt[j % RING][:, D:D + 1].bitcast(i32)).then_inc(y_ok, 1)

            def tiles(i, first, last):
                for j in range(FU):
                    if not (last and j + 1 >= FU):
                        hidden(i, j + 1)
                    result(i, j, not first or j >= RING)

            hidden(0, 0)
            tiles(0, True, False)
            with dve.Fori(1, FT // FU - 1) as i:
                tiles(i, False, False)
            tiles(FT // FU - 1, False, True)

            dve.wait_ge(base_ok, NCH + START)
            for t in range(NT):
                dve.wait_ge(yg_in[t // 4], 16)
                nc.vector.scalar_tensor_tensor(x2[:, t, :], xhat[:, t, 0:D], alpha[:, t:t + 1], x2[:, t, :],
                                               ALU.mult, ALU.add).then_inc(out_ok, 1)

        @block.gpsimd
        def _(pool):
            UB = PH * UNITS
            pool.sem_inc(base_ok, START)
            nc.gpsimd.memset(minus_half[:, :], -0.5)
            nc.gpsimd.memset(eps_col[:, :], EPS)
            more = x2[:, :, :].rearrange("p t d -> p (t d)")[:, 0:(FT - NT) * (D + 1)].rearrange("p (t d) -> p t d", d=D + 1)
            pool.dma_start(pads[:, :].bitcast(i32), pad_ids).then_inc(pad_in, 16)
            pool.dma_start(toks[:, :].bitcast(i32), tok_ids).then_inc(pad_in, 16)
            nc.gpsimd.memset(xhat[:, :, 0:D], 0.0)
            nc.gpsimd.memset(more[:, :, 0:D], 0.0)
            pool.wait_ge(pad_in, 32)
            for rows_of, first, count in ((xhat, 0, NT), (more, NT, FT - NT)):
                last = nc.gpsimd.tensor_copy(rows_of[:, 0:count, D:D + 1].rearrange("p t d -> p (t d)").bitcast(i32),
                                             pads[:, first:first + count].bitcast(i32))
            last.then_inc(setup_pool, 1)
            pool.wait_ge(setup_pool, 1)
            for rows_of, first, count in ((xhat, 0, NT), (more, NT, FT - NT)):
                pool.dma_start(xs_dram[first * P:(first + count) * P, :].rearrange("(u p) d -> p u d", p=P),
                               rows_of[:, 0:count, :]).then_inc(zeroed, 16)

            def rows(k):
                return (xin if k % PH < 2 else x1)[k % 2]

            def prepare_rows(it, k):
                pool.wait_ge(ln_stats, it * PH + (k + 1))
                if k > 0:
                    pool.wait_ge(xn_ok, it * PH + k)
                nc.gpsimd.tensor_tensor(ve[:, :], mv[:, :, 1], eps_col[:, :], ALU.add).then_inc(rstd_own, 1)
                pool.wait_ge(rstd_own, it * PH + (k + 1))
                nc.gpsimd.tensor_tensor(rstd[:, :], ve[:, :], minus_half[:, 0:UNITS], ALU.pow).then_inc(rstd_ok, 1)
                if k == 0:
                    pool.wait_ge(bo_done, 1)
                else:
                    pool.wait_ge(res_ok, it * UB + ((k - 1) * UNITS + START))
                nc.gpsimd.tensor_tensor(xb[k % 2][:, :, :], rows(k)[:, :, :],
                                        bo_eff[:, (k % PH) // 2, :].unsqueeze(1).broadcast_to([P, UNITS, D]),
                                        ALU.add).then_inc(xb_ok, 1)

            def low(it, k, part):
                name = "KQ"[part]
                if k % PH < 2:
                    pool.wait_ge(p_read[pbank(k, name + "r")], read_out(it, k, name + "r"))
                    if k > 0:
                        pool.wait_ge(lo_ok, it * (PH * 2) + (k * 2 - 1 + part))
                    nc.gpsimd.tensor_tensor(p32[part][:, :], p32[part][:, :], t_sin[part][:, :], ALU.add).then_inc(rope_ok, 1)
                    pool.wait_ge(hi_ok, it * (PH * 2) + (k * 2 + part + 1))
                else:
                    pool.wait_ge(p_read[pbank(k, name)], read_out(it, k, name))
                nc.gpsimd.tensor_tensor(plo[part][:, :], p32[part][:, :], phi[part][:, :], ALU.subtract).then_inc(lo_ok, 1)

            prepare_rows(0, 0)
            low(0, 0, 0)
            low(0, 0, 1)
            pool.wait_ge(w1_in, 64)
            for e in range(E):
                last = nc.gpsimd.tensor_tensor(wpack[:, e, 0:F], w1raw[:, e, :], lng[:, e:e + 1].broadcast_to([P, F]), ALU.mult)
            last.then_inc(scaled, 1)

            def deviations(it, k):
                count = [(k - 3) * 5]

                def chained(ins):
                    count[0] += 1
                    ins.then_inc(r_own, 1)
                    pool.wait_ge(r_own, it * 10 + count[0])

                pool.wait_ge(mv3_ok, finished(it, k))
                chained(nc.gpsimd.tensor_tensor(rtmp[:, :], mv3[:, :, 1], eps_col[:, :], ALU.add))
                chained(nc.gpsimd.tensor_tensor(r1[:, :], rtmp[:, :], minus_half[:, :], ALU.pow))
                chained(nc.gpsimd.tensor_tensor(rtmp[:, :], r1[:, :], r1[:, :], ALU.mult))
                chained(nc.gpsimd.tensor_tensor(rtmp[:, :], rtmp[:, :], mv3[:, :, 1], ALU.mult))
                chained(nc.gpsimd.tensor_tensor(rtmp[:, :], rtmp[:, :], eps_col[:, :], ALU.add))
                pool.wait_ge(xhat_ok, finished(it, k) - 1 + START)
                nc.gpsimd.tensor_tensor(r2[:, :], rtmp[:, :], minus_half[:, :], ALU.pow).then_inc(r_ok, 1)

            def add_rows(it, k):
                pool.wait_ge(xl_ok, finished(it, k))
                part = x2[:, bass.ds(it * (2 * UNITS) + (k - 3) * UNITS, UNITS), :]
                nc.gpsimd.tensor_tensor(part, part, xl[:, :, :], ALU.add).then_inc(base_ok, 1)

            def phase(it, k, last=False):
                if not last:
                    prepare_rows(it, k + 1)
                if k > 2:
                    deviations(it, k)
                if not last:
                    low(it, k + 1, 0)
                    low(it, k + 1, 1)
                if k > 2:
                    add_rows(it, k)

            phase(0, 0)
            pool.wait_ge(zeroed, 32)
            nc.gpsimd.tensor_copy(xhat[:, :, D:D + 1].rearrange("p t d -> p (t d)").bitcast(i32), toks[:, :].bitcast(i32)).then_inc(tok_in, 1)
            with pool.Fori(0, ITERS - 1) as it:
                for k in range(1, PH + 1):
                    phase(it, k)
            for k in range(1, PH):
                phase(ITERS - 1, k, k == PH - 1)
            deviations(ITERS - 1, PH)
            add_rows(ITERS - 1, PH)
            pool.wait_ge(xhat_ok, NCH + START)
            pool.wait_ge(tok_in, 1)
            pool.wait_ge(rank_ok, 1)
            for t in range(NT):
                pool.indirect_dma_start(xs_dram, bass.IndirectOffsetOnAxis(ap=pos[:, t:t + 1], axis=0), xhat[:, t, :], None)\
                    .then_inc(scattered, 16)
            with pool.Fori(0, FT // FU) as i:
                for j in range(FU):
                    pool.wait_ge(y_ok, i * FU + (j + 1 + Y0))
                    nc.gpsimd.tensor_tensor(spare_pool[:, j:j + 1], eps_col[:, 0:1], eps_col[:, 0:1], ALU.add).then_inc(yt_taken, 1)
                    pool.indirect_dma_start(ys_dram, bass.IndirectOffsetOnAxis(ap=yt[j % RING][:, D:D + 1].bitcast(i32), axis=0),
                                            yt[j % RING][:, 0:D], None).then_inc(yt_out[j % RING], 16)


def kernel(**inputs):
    import numpy as np
    import concourse.bacc as bacc
    from concourse.bass_utils import run_bass_kernel_spmd

    a = {k: np.asarray(v) for k, v in inputs.items()}
    rot = np.arange(D).reshape(H, 2, HD // 2)[:, ::-1].reshape(D)
    wq, wk = a["L0_attn_wq"], a["L0_attn_wk"]
    wts = np.stack([m.T for m in (wq, wq[rot], wk, wk[rot], a["L0_attn_wv"], a["L0_attn_wo"],
                                  a["L0_xattn_qw"], a["L0_xattn_kw"], a["L0_xattn_vw"], a["L0_xattn_ow"])])
    bq, bk = a["L0_attn_bq"], a["L0_attn_bk"]
    bias_cols = np.stack([bq, bq[rot], bk, bk[rot], a["L0_xattn_qb"], a["L0_xattn_kb"]], axis=1)

    consts = np.zeros((P, C_END), np.float32)
    consts[:, C_ID:C_ID + P] = np.eye(P)
    consts[:, C_TRI:C_TRI + P] = np.triu(np.ones((P, P)), 1)
    inv_freq = (1.0 / 10000.0 ** (np.arange(0, HD, 2, dtype=np.float32) / np.float32(HD))).astype(np.float32)
    freqs = np.arange(S, dtype=np.float32)[:, None] * inv_freq[None, :]
    emb = np.concatenate([freqs, freqs], axis=-1)
    sign = np.where(np.arange(HD) < HD // 2, -1.0, 1.0)
    consts[:, C_COS:C_COS + S] = np.tile(np.cos(emb).T, (H, 1))
    consts[:, C_SIN:C_SIN + S] = np.tile((np.sin(emb) * sign).T, (H, 1))
    for s in range(GH):
        consts[:, C_MASK + s] = (np.arange(P) % 32) // HD == s
    consts[:, C_RANK:C_RANK + E] = E - np.arange(E)
    consts[:, C_SEG:C_SEG + E * NT] = np.arange(E * NT) % NT != 0
    consts[:, C_IOTA:C_IOTA + FT] = np.arange(FT)

    arrays = {
        "x": a["x"].reshape(T, D),
        "tok_ids": np.arange(T, dtype=np.int32).reshape(NT, P).T,
        "pad_ids": T + np.arange(FT * P, dtype=np.int32).reshape(FT, P).T,
        "ctx": a["ctx_1024"].reshape(T, D),
        "mask_q": a["mask_BxSxS2_if1"].reshape(T, S), "mask_k": a["mask_BxSxS2_if1"].transpose(0, 2, 1).reshape(T, S), "wts": wts, "bias_cols": bias_cols,
        "bv_cols": np.stack([a["L0_attn_bv"], a["L0_xattn_vb"]], axis=1),
        "bo_rows": np.stack([a["L0_attn_bo"], a["L0_xattn_ob"]])[None],
        "consts": consts, "centro": a["L0_ffn_centroids"].T, "ln_g": a["L0_ffn_ln_g"].T, "ln_b": a["L0_ffn_ln_b"].T,
        "w1t": a["L0_ffn_w1"].transpose(0, 2, 1), "w2t": a["L0_ffn_w2"].transpose(0, 2, 1),
        "b1c": a["L0_ffn_b1"].reshape(E, FC, P).transpose(2, 0, 1), "b2": a["L0_ffn_b2"],
    }
    nc = bacc.Bacc("TRN2", target_bir_lowering=False, num_devices=1)
    feed, args = {}, []
    for name, value in arrays.items():
        feed[f"in_{name}"] = np.ascontiguousarray(value)
        args.append(nc.dram_tensor(f"in_{name}", value.shape, mybir.dt.from_np(value.dtype), kind="ExternalInput").ap())
    out = nc.dram_tensor("out", (T, D), mybir.dt.float32, kind="ExternalOutput").ap()
    decoder_layer(nc, *args, out)
    r = run_bass_kernel_spmd(nc, [feed], core_ids=[0])
    return r.results[0]["out"].reshape(B, S, D)
```
